# Optimizing a Trainium2 kernel written in Bass

```python
import numpy as np
import jax
import jax.numpy as jnp

def _softmax(x, axis=-1):
    return jax.nn.softmax(x, axis=axis)

def _gelu(x):
    return jax.nn.gelu(x, approximate=True)

def _silu(x):
    return jax.nn.silu(x)

def _sigmoid(x):
    return jax.nn.sigmoid(x)

def _layernorm(x, axis=-1, eps=1e-05):
    m = jnp.mean(x, axis=axis, keepdims=True)
    v = jnp.var(x, axis=axis, keepdims=True)
    return (x - m) / jnp.sqrt(v + eps)

def _scatter_add(tgt, idx, src, axis=0):
    return tgt.at[idx].add(src)

def _segment_sum(src, seg, n):
    return jax.ops.segment_sum(src, seg, n)
kernel_name = 'mk_adaln_d1_jaxref_r4_20a058'

def setup_inputs(seed: int=0):
    np.random.seed(seed)
    _w = jnp.asarray

    def _L0_attn_setup():
        import jax, jax.numpy as jnp
        import numpy as np
        EPS = 1e-06
        key = jax.random.key(seed)
        ks = jax.random.split(key, 8)
        B, S, D = (4, 512, 256)
        sc = 1.0 / np.sqrt(D)
        return {'x_seq': jax.random.normal(ks[0], (B, S, D), jnp.float32), 'Wq': jax.random.normal(ks[1], (D, D), jnp.float32) * sc, 'bq': jax.random.normal(ks[2], (D,), jnp.float32) * 0.01, 'Wk': jax.random.normal(ks[3], (D, D), jnp.float32) * sc, 'bk': jax.random.normal(ks[4], (D,), jnp.float32) * 0.01, 'Wv': jax.random.normal(ks[5], (D, D), jnp.float32) * sc, 'bv': jax.random.normal(ks[6], (D,), jnp.float32) * 0.01, 'gamma': jnp.float32(0.9)}
    _L0_attn_in = _L0_attn_setup()

    def _L0_ffn_setup():
        import jax, jax.numpy as jnp
        import numpy as np
        D_MODEL, D_FF, N_EXP = (256, 1024, 8)
        key = jax.random.key(seed)
        ks = jax.random.split(key, 8)
        s = lambda fan_in: 1.0 / np.sqrt(fan_in)
        x = jax.random.normal(ks[0], (4, 512, D_MODEL), dtype=jnp.float32)
        Wr = jax.random.uniform(ks[1], (N_EXP, D_MODEL), jnp.float32, -s(D_MODEL), s(D_MODEL))
        br = jax.random.uniform(ks[2], (N_EXP,), jnp.float32, -s(D_MODEL), s(D_MODEL))
        W1 = jax.random.uniform(ks[3], (N_EXP, D_FF, D_MODEL), jnp.float32, -s(D_MODEL), s(D_MODEL))
        b1 = jax.random.uniform(ks[4], (N_EXP, D_FF), jnp.float32, -s(D_MODEL), s(D_MODEL))
        W2 = jax.random.uniform(ks[5], (N_EXP, D_MODEL, D_FF), jnp.float32, -s(D_FF), s(D_FF))
        b2 = jax.random.uniform(ks[6], (N_EXP, D_MODEL), jnp.float32, -s(D_FF), s(D_FF))
        return {'x': x, 'Wr': Wr, 'br': br, 'W1': W1, 'b1': b1, 'W2': W2, 'b2': b2}
    _L0_ffn_in = _L0_ffn_setup()
    _L0_c = _w((lambda *s: np.random.randn(*s).astype(np.float32) * 0.05)(2, 256))
    _L0_wmod = _w((lambda *s: np.random.randn(*s).astype(np.float32) * 0.05)(256, 6 * 256) * 256 ** (-0.5))
    _d = {'L0_attn_x_seq': _L0_attn_in['x_seq'], 'L0_attn_Wq': _L0_attn_in['Wq'], 'L0_attn_bq': _L0_attn_in['bq'], 'L0_attn_Wk': _L0_attn_in['Wk'], 'L0_attn_bk': _L0_attn_in['bk'], 'L0_attn_Wv': _L0_attn_in['Wv'], 'L0_attn_bv': _L0_attn_in['bv'], 'L0_attn_gamma': _L0_attn_in['gamma'], 'L0_ffn_Wr': _L0_ffn_in['Wr'], 'L0_ffn_br': _L0_ffn_in['br'], 'L0_ffn_W1': _L0_ffn_in['W1'], 'L0_ffn_b1': _L0_ffn_in['b1'], 'L0_ffn_W2': _L0_ffn_in['W2'], 'L0_ffn_b2': _L0_ffn_in['b2'], 'L0_c': _L0_c, 'L0_wmod': _L0_wmod}
    _x0 = _d['L0_attn_x_seq']
    _d['L0_attn_x_seq'] = jax.random.normal(jax.random.fold_in(jax.random.key(seed), 1), (2, 2048, 256), dtype=_x0.dtype)
    del _x0
    return _d

def reference(L0_attn_x_seq, L0_attn_Wq, L0_attn_bq, L0_attn_Wk, L0_attn_bk, L0_attn_Wv, L0_attn_bv, L0_attn_gamma, L0_ffn_Wr, L0_ffn_br, L0_ffn_W1, L0_ffn_b1, L0_ffn_W2, L0_ffn_b2, L0_c, L0_wmod):

    def _L0_attn_ref(x_seq, Wq, bq, Wk, bk, Wv, bv, gamma):
        import jax, jax.numpy as jnp
        import numpy as np
        EPS = 1e-06
        B, S, D = x_seq.shape
        q = jax.nn.relu(jnp.einsum('bsd,ed->bse', x_seq, Wq) + bq)
        k = jax.nn.relu(jnp.einsum('bsd,ed->bse', x_seq, Wk) + bk)
        v = jnp.einsum('bsd,ed->bse', x_seq, Wv) + bv

        def step(carry, qkv):
            s, z = carry
            q_t, k_t, v_t = qkv
            s = gamma * s + jnp.einsum('bi,bj->bij', k_t, v_t)
            z = gamma * z + k_t
            num = jnp.einsum('bi,bij->bj', q_t, s)
            denom = jnp.sum(q_t * z, axis=-1, keepdims=True) + EPS
            return ((s, z), num / denom)
        s0 = jnp.zeros((B, D, D), x_seq.dtype)
        z0 = jnp.zeros((B, D), x_seq.dtype)
        qkv = (jnp.swapaxes(q, 0, 1), jnp.swapaxes(k, 0, 1), jnp.swapaxes(v, 0, 1))
        _, ys = jax.lax.scan(step, (s0, z0), qkv)
        return jnp.swapaxes(ys, 0, 1)

    def _L0_ffn_ref(x, Wr, br, W1, b1, W2, b2):
        import jax, jax.numpy as jnp
        import numpy as np
        D_MODEL, D_FF, N_EXP = (256, 1024, 8)
        B, S, D = x.shape
        xf = x.reshape(-1, D)
        logits = xf @ Wr.T + br
        expert_idx = jnp.argmax(logits, axis=-1)
        h = jax.nn.relu(jnp.einsum('td,efd->etf', xf, W1) + b1[:, None, :])
        y = jnp.einsum('etf,edf->etd', h, W2) + b2[:, None, :]
        out = y[expert_idx, jnp.arange(xf.shape[0])]
        return out.reshape(B, S, D)
    x = L0_attn_x_seq
    mod = (_silu(L0_c) @ L0_wmod).reshape(L0_c.shape[0], 6, 1, -1)
    sa, ca, ga, sb, cb, gb = (mod[:, 0], mod[:, 1], mod[:, 2], mod[:, 3], mod[:, 4], mod[:, 5])
    ga = (2 * (ga >= 0) - 1) * jnp.maximum(jnp.abs(ga), 0.25)
    gb = (2 * (gb >= 0) - 1) * jnp.maximum(jnp.abs(gb), 0.25)
    h = _layernorm(x, axis=-1) * (1 + ca) + sa
    x = x + ga * _L0_attn_ref(h, L0_attn_Wq, L0_attn_bq, L0_attn_Wk, L0_attn_bk, L0_attn_Wv, L0_attn_bv, L0_attn_gamma)
    h = _layernorm(x, axis=-1) * (1 + cb) + sb
    x = x + gb * _L0_ffn_ref(h, L0_ffn_Wr, L0_ffn_br, L0_ffn_W1, L0_ffn_b1, L0_ffn_W2, L0_ffn_b2)
    return x

_drawn_inputs = setup_inputs


def setup_inputs(seed=0):
    import zlib

    import numpy as np

    out = dict(_drawn_inputs(seed))
    spreads = {}
    factors = {'L0_attn_Wq': 5.674,
     'L0_attn_bq': 8.0,
     'L0_attn_Wk': 4.985,
     'L0_attn_bk': 8.0,
     'L0_attn_bv': 8.0,
     'L0_ffn_br': 3.467,
     'L0_ffn_b1': 8.0,
     'L0_ffn_b2': 8.0}
    for name, (base, spread) in spreads.items():
        noise = np.random.default_rng([zlib.crc32(name.encode()), seed]).standard_normal(out[name].shape)
        drawn = base * np.exp(spread * noise) if base else spread * noise
        out[name] = jnp.asarray(drawn.astype(out[name].dtype))
    for name, factor in factors.items():
        out[name] = (out[name] * factor).astype(out[name].dtype)
    return out
```

```python
from contextlib import ExitStack

import numpy as np

import concourse.bass as bass
from concourse import mybir

F32 = mybir.dt.float32
I32 = mybir.dt.int32
ALU = mybir.AluOpType
ACT = mybir.ActivationFunctionType
AX_X = mybir.AxisListType.X

P = 128
B, S, D = 2, 2048, 256
DK = D // P
NE, F = 8, 1024
FK = F // P
NTOK = B * S
NCH = NTOK // P
NT = NCH + NE - 1
DZ = D + 1
NPOW = 2 * P + 2
LN_EPS, DEN_EPS = 1e-5, 1e-6
INIT = B * (DK + 1) + 3

LOAD, STATS, NORM, XPOSE, PROJ, SCORE, ATTEND, NORM2, XPOSE2, LOGIT = -6, -3, -2, -1, 0, 1, 2, 3, 4, 5
COLS = {}
_at = 0
for _name, _n in (("ident", P), ("before", P), ("ones", P), ("causal", P), ("weight8", NE),
                  ("bounds", NCH), ("tile_no", NT), ("slot_no", P), ("token_less", NCH)):
    COLS[_name] = (_at, _at + _n)
    _at += _n
NCONST = _at


def constants():
    p = np.arange(P)
    c = np.zeros((P, NCONST), np.float32)

    def put(name, value):
        a, b = COLS[name]
        c[:, a:b] = value

    put("ident", np.eye(P))
    put("before", p[:, None] < p[None, :])
    put("ones", 1.0)
    put("causal", p[:, None] <= p[None, :])
    put("weight8", NE - np.arange(NE)[None, :])
    put("bounds", (P * np.arange(NCH))[None, :])
    put("tile_no", np.arange(NT)[None, :])
    put("slot_no", p[None, :])
    n = np.arange(NCH)
    put("token_less", (n % B)[None, :] * S + (n // B)[None, :] * P + p[:, None] - NTOK)
    e = np.zeros((P, NPOW), np.int32)
    e[:, 0:P] = np.maximum(p[None, :] - p[:, None], 0)
    e[:, P:2 * P] = p[None, :] + 1
    e[:, 2 * P] = P - 1 - p
    e[:, 2 * P + 1] = P
    return c, e


def need(eng, sem, count):
    if isinstance(count, int) and count <= 0:
        return
    eng.wait_ge(sem, count)


def slots(eng, unroll, first, loop, last, slot):
    for k in range(first, loop[0]):
        for u in range(unroll):
            slot(k, u)
    with eng.Fori(loop[0], loop[1], 1) as k:
        for u in range(unroll):
            slot(k, u)
    for k in range(loop[1], last + 1):
        for u in range(unroll):
            slot(k, u)


def item(k, u, lag, unroll, count):
    q, r = divmod(u - lag, unroll)
    g = k + q
    n = g * unroll + r
    if isinstance(n, int) and not 0 <= n < count:
        return None
    return n, g, r


ATT = (B, -3, (4, 13), 18)
FFN = (3, -1, (2, 12), 13)


def build(nc, x, wqkv, bqk, bvb, gamma, wr, brb, w1, b1, w2, b2b, c_t, wmod, consts, exps, out):
    rows = nc.dram_tensor("token_rows", [NTOK, 2 * D], F32, kind="Internal").ap()
    with ExitStack() as ctx:
        def sb(name, shape, dt=F32):
            return ctx.enter_context(nc.sbuf_tensor(name, shape, dt))

        def sem(name):
            return ctx.enter_context(nc.semaphore(name))

        bank = {n: ctx.enter_context(nc.psum_tensor(f"ps_{n}", [P, 512], F32))
                for n in ("o", "kv0", "kv1", "qk", "va", "x", "h", "k")}

        w1_sb = sb("w1_sb", [P, NE, DK, F])
        w2_sb = sb("w2_sb", [P, NE, FK, D])
        cst = sb("cst", [P, NCONST])
        wqkv_sb = sb("wqkv_sb", [P, 3, DK, D])
        bqk_sb = sb("bqk_sb", [P, 2, DK])
        bv_sb = sb("bv_sb", [P, D])
        wr_sb = sb("wr_sb", [P, DK, NE])
        br_sb = sb("br_sb", [P, NE])
        b1_sb = sb("b1_sb", [P, NE, FK])
        b2_sb = sb("b2_sb", [P, NE, D])
        mod_t = sb("mod_t", [P, 2 * DK, B])
        gate_a = sb("gate_a", [P, B, D])
        shift_b = sb("shift_b", [P, B, D])
        scale_b = sb("scale_b", [P, B, D])
        gate_b = sb("gate_b", [P, B, D])
        logits = sb("logits", [P, NCH, NE])
        power = sb("power", [P, NPOW])
        decay = sb("decay", [P, P])
        slot_token = sb("slot_token", [P, NT], I32)
        slot_late = sb("slot_late", [P, NT])
        slot_early = sb("slot_early", [P, NT])
        tile_expert = sb("tile_expert", [P, NT], I32)

        arena = sb("arena", [P, 9216])
        at = [0]

        def cut(*shape):
            n = int(np.prod(shape))
            v = arena[:, at[0]:at[0] + n]
            at[0] += n
            assert at[0] <= 9216, at
            if len(shape) == 2:
                v = v.rearrange("p (a b) -> p a b", a=shape[0])
            if len(shape) == 3:
                v = v.rearrange("p (a b c) -> p a b c", a=shape[0], b=shape[1])
            return v

        x_sb = cut(B, 4, D)
        xn1 = cut(B, D)
        h_t = cut(B, DK, P)
        q_t = cut(B, DK, P)
        k_t = cut(B, DK, P)
        qg_t = cut(B, DK, P)
        kg = cut(B, D)
        v_ext = cut(B, DZ + 1)
        att = cut(B, P)
        x1_sb = cut(B, D)
        xn2 = cut(B, D)
        h2 = cut(B, D)
        h2_t = cut(B, DK, P)
        state = cut(B, DK, DZ + 1)
        small = sb("small", [P, 64])
        st1, st2 = sb("st1", [P, B, 6]), sb("st2", [P, B, 6])
        mv1, mv2 = sb("mv1", [P, B, 2]), sb("mv2", [P, B, 2])
        rs1, rs2 = sb("rs1", [P, B, 4]), sb("rs2", [P, B, 4])
        den = sb("den", [P, B, 2])
        attended = sb("attended", [P, B, D])
        att_end = at[0]

        at[0] = 0
        tok = cut(3, 2 * D)
        tok_t = cut(3, DK, P)
        hid = cut(F)
        hid_t = cut(FK, P)
        done_rows = cut(3, D)
        gate_now = cut(3, D)
        gate_tmp = cut(3, D)
        b2_now = cut(3, D)
        b1_now = cut(3, FK)
        assert at[0] <= 9216
        idx_in = sb("idx_in", [P, 3], I32)
        idx_out = sb("idx_out", [P, 3], I32)
        flag_now = sb("flag_now", [P, 3, 2])

        wmod_sb = w2_sb[:, 6:8].rearrange("p e f d -> p (e f d)")[:, 0:DK * 6 * D].rearrange(
            "p (k m) -> p k m", k=DK)
        w1_tail = w1_sb[:, 7].rearrange("p k f -> p (k f)")
        c_sb = w1_tail[:, 0:4].rearrange("p (k b) -> p k b", k=DK)
        c_exp = w1_tail[:, 4:8].rearrange("p (k b) -> p k b", k=DK)
        c_silu = w1_tail[:, 8:12].rearrange("p (k b) -> p k b", k=DK)
        c_wide = w1_tail[:, 128:640].rearrange("p (k b m) -> p k b m", k=DK, b=B)
        exps_sb = w1_tail[:, 640:640 + NPOW].bitcast(I32)
        bit_sb = w1_tail[:, 900:900 + NPOW].bitcast(I32)
        powg_sb = w1_tail[:, 1160:1160 + NPOW]
        sign_sb = w1_tail[:, 1420:1420 + D]
        mag_sb = w1_tail[:, 1676:1676 + D]
        raw_sb = w2_sb[:, 7, FK - 1, :]
        gpow = small[:, 0:8]

        def con(name):
            a, b = COLS[name]
            return cst[:, a:b]

        ident = con("ident")

        s_const, s_x = sem("constants_landed"), [sem(f"x_landed_{b}") for b in range(B)]
        s_cmod, s_gamma, s_wqkv, s_misc = (sem("c_wmod_landed"), sem("gamma_landed"), sem("wqkv_landed"),
                                           sem("biases_landed"))
        s_experts = sem("expert_weights_landed")
        s_cexp, s_csilu, s_modt, s_modt_ready = (sem("c_exp_ready"), sem("c_silu_ready"), sem("mod_t_done"),
                                                 sem("mod_t_ready"))
        s_modb, s_modb_ready, s_setup = sem("mod_rows_done"), sem("mod_rows_ready"), sem("setup_step")
        s_pow = sem("power_step")
        s_marks = sem("marks")
        s_decay, s_init = sem("decay_ready"), sem("state_cleared")
        (s_st1, s_mv1, s_rs1s, s_rs1, s_xn1, s_xt, s_ht) = map(sem, (
            "stats1", "mean_var1", "rstd1_step", "rstd1", "xn1_ready", "x_transposed", "h_t_ready"))
        (s_qkp, s_vp, s_q, s_k, s_qg, s_v) = map(sem, (
            "qk_projected", "v_projected", "q_ready", "k_ready", "qg_ready", "v_ready"))
        (s_kx, s_kg, s_sc, s_att) = map(sem, ("k_transposed", "kg_ready", "scores_done", "att_ready"))
        (s_o, s_kv, s_state, s_den, s_rden, s_atn, s_x1) = map(sem, (
            "attended_done", "kv_done", "state_ready", "den_ready", "rden_ready", "attended_ready", "x1_ready"))
        (s_st2, s_mv2, s_rs2s, s_rs2, s_xn2, s_h2s, s_h2) = map(sem, (
            "stats2", "mean_var2", "rstd2_step", "rstd2", "xn2_ready", "h2_step", "h2_ready"))
        (s_h2x, s_h2t, s_lg, s_lgr) = map(sem, ("h2_transposed", "h2_t_ready", "logits_done", "logits_ready"))
        s_sx = [sem(f"x1_stored_{b}") for b in range(B)]
        s_sh = [sem(f"h2_stored_{b}") for b in range(B)]
        s_route, s_chosen, s_rank, s_bits, s_ids, s_routed = map(sem, (
            "route_step", "chosen_ready", "ranks_done", "slots_hot", "ids_done", "routed"))
        s_in = [sem(f"tokens_gathered_{r}") for r in range(3)]
        s_out = [sem(f"rows_scattered_{r}") for r in range(3)]
        (s_idx, s_prep, s_preps, s_tx, s_tt, s_hp, s_ha, s_hd, s_hx, s_hta, s_htd, s_y, s_ys, s_done) = map(sem, (
            "index_copied", "tile_constants_ready", "tile_constants_step", "tokens_transposed", "tok_t_ready",
            "hidden_done", "hidden_ready_act", "hidden_ready_dve", "hidden_transposed", "hid_t_ready_act",
            "hid_t_ready_dve", "y_done", "y_step", "rows_done"))

        block = ctx.enter_context(nc.Block())

        def att_item(k, u, lag):
            return item(k, u, lag, B, NCH)

        def ffn_item(k, u, lag):
            return item(k, u, lag, 3, NT)

        def alone(eng, *waits):
            for w, c in waits:
                need(eng, w, c)
                eng.sem_inc(s_marks, 1)

        def token_row(g, r):
            return r * S + g * P

        @block.sync
        def _(sp):
            sp.dma_start(c_sb, c_t).then_inc(s_cmod, 16)
            sp.dma_start(wmod_sb, wmod).then_inc(s_cmod, 16)
            sp.dma_start(cst[:], consts).then_inc(s_const, 16)

            def slot(k, u):
                if it := att_item(k, u, LOAD):
                    n, g, r = it
                    alone(sp, (s_x[r], g * 16), (s_x1, n - 7))
                    sp.dma_start(x_sb[:, r, bass.ds(g % 4, 1), :].rearrange("p a d -> p (a d)"),
                                 x[bass.ds(token_row(g, r), P), :]).then_inc(s_x[r], 16)
                    if isinstance(n, int) and n == 1:
                        sp.dma_start(wqkv_sb[:], wqkv).then_inc(s_wqkv, 16)
                        sp.dma_start(bqk_sb[:], bqk).then_inc(s_wqkv, 16)
                        sp.dma_start(bv_sb[:], bvb).then_inc(s_misc, 16)
                        sp.dma_start(wr_sb[:], wr).then_inc(s_misc, 16)
                        sp.dma_start(br_sb[:], brb).then_inc(s_misc, 16)
                        sp.dma_start(b1_sb[:], b1).then_inc(s_misc, 16)
                        sp.dma_start(b2_sb[:], b2b).then_inc(s_misc, 16)
                if it := att_item(k, u, ATTEND):
                    n, g, r = it
                    alone(sp, (s_sx[r], g * 16), (s_x1, n + 1))
                    sp.dma_start(rows[bass.ds(token_row(g, r), P), 0:D], x1_sb[:, r, :]).then_inc(s_sx[r], 16)
                if it := att_item(k, u, NORM2):
                    n, g, r = it
                    alone(sp, (s_sh[r], g * 16), (s_h2, n + 1))
                    sp.dma_start(rows[bass.ds(token_row(g, r), P), D:2 * D], h2[:, r, :]).then_inc(s_sh[r], 16)

            slots(sp, *ATT, slot)

        @block.gpsimd
        def _(pool):
            pool.dma_start(exps_sb, exps).then_inc(s_gamma, 16)
            pool.dma_start(gpow[:, 0:1], gamma).then_inc(s_gamma, 16)
            for b in range(B):
                for k in range(DK):
                    pool.memset(state[:, b, k, :], 0.0).then_inc(s_init, 1)
                pool.memset(v_ext[:, b, D:DZ], 1.0).then_inc(s_init, 1)

            def inverse_deviation(n, r, s_mv, mv, rs, s_step, s_free, s_ready):
                pool.wait_ge(s_mv, n + 1)
                need(pool, s_free, n - 1)
                pool.tensor_tensor(rs[:, r, 0:1], mv[:, r, 1:2], fixed[:, 1:2], ALU.add).then_inc(s_step, 1)
                pool.wait_ge(s_step, 3 * n + 1)
                pool.tensor_tensor(rs[:, r, 1:2], rs[:, r, 0:1], fixed[:, 0:1], ALU.pow).then_inc(s_step, 1)
                pool.wait_ge(s_step, 3 * n + 2)
                pool.tensor_tensor(rs[:, r, 3:4], mv[:, r, 0:1], rs[:, r, 1:2], ALU.mult).then_inc(s_step, 1)
                pool.wait_ge(s_step, 3 * n + 3)
                pool.tensor_tensor(rs[:, r, 2:3], rs[:, r, 3:4], fixed[:, 2:3], ALU.mult).then_inc(s_ready, 1)

            fixed = small[:, 8:11]
            for i, value in enumerate((-0.5, LN_EPS, -1.0)):
                pool.memset(fixed[:, i:i + 1], value).then_inc(s_init, 1)
            pool.wait_ge(s_init, INIT)

            def slot(k, u):
                if it := att_item(k, u, NORM):
                    n, g, r = it
                    inverse_deviation(n, r, s_mv1, mv1, rs1, s_rs1s, s_xn1, s_rs1)
                if it := att_item(k, u, NORM2):
                    n, g, r = it
                    inverse_deviation(n, r, s_mv2, mv2, rs2, s_rs2s, s_xn2, s_rs2)
                    if isinstance(n, int) and n == 0:
                        pool.wait_ge(s_modb_ready, B)
                    pool.wait_ge(s_xn2, n + 1)
                    need(pool, s_h2x, n - 1)
                    need(pool, s_sh[r], 16 * g)
                    pool.tensor_tensor(xn2[:, r, :], xn2[:, r, :], scale_b[:, r, :], ALU.mult).then_inc(s_h2s, 1)
                    pool.wait_ge(s_h2s, n + 1)
                    pool.tensor_tensor(h2[:, r, :], xn2[:, r, :], shift_b[:, r, :], ALU.add).then_inc(s_h2, 1)
                if it := att_item(k, u, PROJ):
                    n, g, r = it
                    if isinstance(n, int) and n == 0:
                        pool.wait_ge(s_decay, 1)
                    pool.wait_ge(s_q, n + 1)
                    need(pool, s_o, n - 1)
                    pool.tensor_tensor(qg_t[:, r], q_t[:, r],
                                       power[:, P:2 * P].unsqueeze(1).to_broadcast([P, DK, P]),
                                       ALU.mult).then_inc(s_qg, 1)

            slots(pool, *ATT, slot)

            for b in range(B):
                pool.wait_ge(s_sx[b], 16 * (NCH // B))
                pool.wait_ge(s_sh[b], 16 * (NCH // B))
            pool.wait_ge(s_routed, 1)
            pool.memset(tok, 0.0).then_inc(s_idx, 1)
            pool.wait_ge(s_idx, 1)

            def slot(k, u):
                if it := ffn_item(k, u, 1):
                    n, g, r = it
                    need(pool, s_out[r], 16 * g)
                    pool.tensor_copy(idx_out[:, r:r + 1], slot_token[:, bass.ds(n, 1)]).then_inc(s_preps, 1)
                    alone(pool, (s_preps, n + 1), (s_done, n + 1))
                    pool.indirect_dma_start(out, bass.IndirectOffsetOnAxis(idx_out[:, r:r + 1], 0),
                                            done_rows[:, r, :], None, bounds_check=NTOK - 1,
                                            oob_is_err=False).then_inc(s_out[r], 16)
                if it := ffn_item(k, u, -2):
                    n, g, r = it
                    need(pool, s_done, n - 2)
                    pool.tensor_copy(idx_in[:, r:r + 1], slot_token[:, bass.ds(n, 1)]).then_inc(s_idx, 1)
                    alone(pool, (s_idx, n + 2), (s_in[r], 16 * g))
                    pool.indirect_dma_start(tok[:, r, :], None, rows,
                                            bass.IndirectOffsetOnAxis(idx_in[:, r:r + 1], 0),
                                            bounds_check=NTOK - 1, oob_is_err=False).then_inc(s_in[r], 16)
                    e = pool.value_load(tile_expert[0:1, bass.ds(n, 1)], min_val=0, max_val=NE - 1)
                    pool.tensor_copy(b1_now[:, r, :], b1_sb[:, bass.ds(e, 1), :].rearrange("p a f -> p (a f)"))
                    pool.tensor_copy(b2_now[:, r, :], b2_sb[:, bass.ds(e, 1), :].rearrange("p a d -> p (a d)"))
                    pool.tensor_copy(flag_now[:, r, 0:1], slot_early[:, bass.ds(n, 1)]).then_inc(s_prep, 1)
                    pool.tensor_copy(flag_now[:, r, 1:2], slot_late[:, bass.ds(n, 1)]).then_inc(s_prep, 1)
                    pool.wait_ge(s_prep, 5 * n + 2)
                    pool.tensor_tensor(gate_now[:, r, :], gate_b[:, 0, :], flag_now[:, r, 0:1].to_broadcast([P, D]),
                                       ALU.mult).then_inc(s_prep, 1)
                    pool.tensor_tensor(gate_tmp[:, r, :], gate_b[:, 1, :], flag_now[:, r, 1:2].to_broadcast([P, D]),
                                       ALU.mult).then_inc(s_prep, 1)
                    pool.wait_ge(s_prep, 5 * n + 4)
                    pool.tensor_tensor(gate_now[:, r, :], gate_now[:, r, :], gate_tmp[:, r, :],
                                       ALU.add).then_inc(s_prep, 1)

            slots(pool, *FFN, slot)
            for r in range(3):
                pool.wait_ge(s_out[r], 16 * (NT // 3))

        @block.scalar
        def _(act):
            act.wait_ge(s_cmod, 32)
            act.activation(c_exp, c_sb, ACT.Exp, scale=-1.0).then_inc(s_cexp, 1)
            for e in range(NE - 2):
                act.dma_start(w1_sb[:, e], w1[e]).then_inc(s_experts, 16)
                act.dma_start(w2_sb[:, e], w2[e]).then_inc(s_experts, 16)

            def slot(k, u):
                if it := att_item(k, u, SCORE):
                    n, g, r = it
                    act.wait_ge(s_kx, n + 1)
                    need(act, s_kv, n - 1)
                    act.activation(kg[:, r, :], bank["k"][:, 0:D], ACT.Copy,
                                   scale=power[:, 2 * P:2 * P + 1]).then_inc(s_kg, 1)
                if it := att_item(k, u, NORM2):
                    n, g, r = it
                    act.wait_ge(s_rs2, n + 1)
                    need(act, s_h2, n - 1)
                    act.activation(xn2[:, r, :], x1_sb[:, r, :], ACT.Identity, bias=rs2[:, r, 2:3],
                                   scale=rs2[:, r, 1:2]).then_inc(s_xn2, 1)
                if it := att_item(k, u, PROJ):
                    n, g, r = it
                    act.wait_ge(s_qkp, n + 1)
                    need(act, s_sc, n - 1)
                    need(act, s_qg, n - 1)
                    for h in range(DK):
                        last = act.activation(q_t[:, r, h, :], bank["qk"][:, h * P:(h + 1) * P], ACT.Relu,
                                              bias=bqk_sb[:, 0, h:h + 1])
                    last.then_inc(s_q, 1)
                    for h in range(DK):
                        last = act.activation(k_t[:, r, h, :], bank["qk"][:, D + h * P:D + (h + 1) * P], ACT.Relu,
                                              bias=bqk_sb[:, 1, h:h + 1])
                    last.then_inc(s_k, 1)
                if it := att_item(k, u, XPOSE2):
                    n, g, r = it
                    act.wait_ge(s_h2x, n + 1)
                    need(act, s_lg, n - 1)
                    act.activation(h2_t[:, r], bank["h"][:, 0:D].rearrange("p (k t) -> p k t", k=DK),
                                   ACT.Copy).then_inc(s_h2t, 1)
                if it := att_item(k, u, XPOSE):
                    n, g, r = it
                    act.wait_ge(s_xt, n + 1)
                    if isinstance(n, int) and n == 0:
                        act.wait_ge(s_modt_ready, 1)
                    need(act, s_vp, n - 1)
                    for h in range(DK):
                        last = act.activation(h_t[:, r, h, :], bank["x"][:, h * P:(h + 1) * P], ACT.Identity,
                                              bias=mod_t[:, h, r:r + 1], scale=mod_t[:, DK + h, r:r + 1])
                    last.then_inc(s_ht, 1)
                if it := att_item(k, u, NORM):
                    n, g, r = it
                    act.wait_ge(s_rs1, n + 1)
                    need(act, s_xt, n - 1)
                    act.activation(xn1[:, r, :], x_sb[:, r, bass.ds(g % 4, 1), :].rearrange("p a d -> p (a d)"),
                                   ACT.Identity, bias=rs1[:, r, 2:3], scale=rs1[:, r, 1:2]).then_inc(s_xn1, 1)
                if isinstance(k, int) and (k, u) == (2, 0):
                    act.wait_ge(s_modb_ready, B)
                    act.wait_ge(s_decay, 1)
                    act.wait_ge(s_modb, 2)
                    for e in range(NE - 2, NE):
                        act.dma_start(w1_sb[:, e], w1[e]).then_inc(s_experts, 16)
                        act.dma_start(w2_sb[:, e], w2[e]).then_inc(s_experts, 16)

            slots(act, *ATT, slot)

            act.wait_ge(s_idx, 1)

            def slot(k, u):
                if it := ffn_item(k, u, 0):
                    n, g, r = it
                    act.wait_ge(s_hp, 2 * n + 1)
                    need(act, s_hx, 2 * n)
                    act.activation(hid[:, 0:512], bank["qk"][:], ACT.Copy).then_inc(s_ha, 1)
                    act.wait_ge(s_hx, 2 * n + 1)
                    act.wait_ge(s_prep, 5 * n + 5)
                    need(act, s_y, n)
                    for f in range(FK // 2):
                        last = act.activation(hid_t[:, f, :], bank["kv0"][:, f * P:(f + 1) * P], ACT.Relu,
                                              bias=b1_now[:, r, f:f + 1])
                    last.then_inc(s_hta, 1)
                if it := ffn_item(k, u, -1):
                    n, g, r = it
                    act.wait_ge(s_tx, n + 1)
                    need(act, s_hp, 2 * (n - 2))
                    act.activation(tok_t[:, r], bank["h"][:, 0:D].rearrange("p (k t) -> p k t", k=DK),
                                   ACT.Copy).then_inc(s_tt, 1)

            slots(act, *FFN, slot)

        @block.vector
        def _(dve):
            steps = [0]

            def step(ins):
                steps[0] += 1
                ins.then_inc(s_setup, 1)
                dve.wait_ge(s_setup, steps[0])

            dve.wait_ge(s_cexp, 1)
            step(dve.tensor_scalar(c_exp, c_exp, 1.0, None, ALU.add))
            step(dve.reciprocal(c_exp, c_exp))
            step(dve.tensor_tensor(c_silu, c_sb, c_exp, ALU.mult))
            dve.wait_ge(s_const, 16)
            for k in range(DK):
                for b in range(B):
                    last = dve.tensor_scalar(c_wide[:, k, b, :], con("ones"), c_silu[:, k, b:b + 1], None, ALU.mult)
            last.then_inc(s_csilu, 1)

            def stats(n, r, src, st, mv, s_st, s_mv, s_free):
                need(dve, s_free, n - 1)
                dve.bn_stats(st[:, r, :], src).then_inc(s_st, 1)
                alone(dve, (s_st, n + 1))
                dve.bn_aggr(mv[:, r, :], st[:, r, :]).then_inc(s_mv, 1)

            def first_stats(k, u):
                if it := att_item(k, u, STATS):
                    n, g, r = it
                    dve.wait_ge(s_x[r], 16 * (g + 1))
                    stats(n, r, x_sb[:, r, bass.ds(g % 4, 1), :].rearrange("p a d -> p (a d)"), st1, mv1,
                          s_st1, s_mv1, s_rs1)

            def mod_widths():
                dve.wait_ge(s_modt, 1)
                m = bank["k"][:, 0:4 * B].rearrange("p (m b) -> p m b", b=B)
                dve.tensor_copy(mod_t[:, 0:DK, :], m[:, 0:DK, :])
                dve.tensor_scalar(mod_t[:, DK:2 * DK, :], m[:, DK:2 * DK, :], 1.0, None,
                                  ALU.add).then_inc(s_modt_ready, 1)

            def powers():
                done = [0]

                def link(ins):
                    done[0] += 1
                    ins.then_inc(s_pow, 1)
                    dve.wait_ge(s_pow, done[0])

                dve.wait_ge(s_gamma, 32)
                link(dve.memset(power[:], 1.0))
                for b in range(8):
                    link(dve.tensor_scalar(bit_sb, exps_sb, 1 << b, None, ALU.bitwise_and))
                    link(dve.tensor_scalar(powg_sb, power[:], gpow[:, b:b + 1], None, ALU.mult))
                    link(dve.copy_predicated(power[:], bit_sb, powg_sb))
                    if b < 7:
                        link(dve.tensor_tensor(gpow[:, b + 1:b + 2], gpow[:, b:b + 1], gpow[:, b:b + 1], ALU.mult))
                dve.tensor_tensor(decay[:], power[:, 0:P], con("causal"), ALU.mult).then_inc(s_decay, 1)
                dve.wait_ge(s_decay, 1)

            def mod_rows():
                def gate(to, src):
                    step(dve.tensor_scalar(sign_sb, src, 0.0, 2.0, ALU.is_ge, ALU.mult))
                    step(dve.tensor_copy(raw_sb, src))
                    step(dve.scalar_tensor_tensor(mag_sb, raw_sb, -1.0, raw_sb, ALU.mult, ALU.max))
                    step(dve.tensor_scalar(mag_sb, mag_sb, 0.25, None, ALU.max))
                    step(dve.scalar_tensor_tensor(to, sign_sb, -1.0, mag_sb, ALU.add, ALU.mult))

                for b, (lo, hi) in enumerate((("kv0", "kv1"), ("o", "h"))):
                    dve.wait_ge(s_modb, b + 1)
                    gate(gate_a[:, b, :], bank[lo][:, 0:D])
                    dve.tensor_copy(shift_b[:, b, :], bank[lo][:, D:2 * D])
                    dve.tensor_scalar(scale_b[:, b, :], bank[hi][:, 0:D], 1.0, None, ALU.add)
                    gate(gate_b[:, b, :], bank[hi][:, D:2 * D])
                    dve.memset(small[:, 16:17], 0.0).then_inc(s_modb_ready, 1)

            def slot(k, u):
                if it := att_item(k, u, ATTEND):
                    n, g, r = it
                    dve.wait_ge(s_o, n + 1)
                    dve.tensor_scalar(den[:, r, 0:1], bank["o"][:, D:DZ], DEN_EPS, None, ALU.add).then_inc(s_den, 1)
                    dve.wait_ge(s_den, n + 1)
                    dve.reciprocal(den[:, r, 1:2], den[:, r, 0:1]).then_inc(s_rden, 1)
                    dve.wait_ge(s_rden, n + 1)
                    dve.scalar_tensor_tensor(attended[:, r, :], bank["o"][:, 0:D], den[:, r, 1:2], gate_a[:, r, :],
                                             ALU.mult, ALU.mult).then_inc(s_atn, 1)
                    dve.wait_ge(s_atn, n + 1)
                    need(dve, s_sx[r], 16 * g)
                    need(dve, s_xn2, n - 1)
                    dve.tensor_tensor(x1_sb[:, r, :], attended[:, r, :],
                                      x_sb[:, r, bass.ds(g % 4, 1), :].rearrange("p a d -> p (a d)"),
                                      ALU.add).then_inc(s_x1, 1)
                    dve.wait_ge(s_kv, n + 1)
                    for h in range(DK):
                        last = dve.scalar_tensor_tensor(state[:, r, h, 0:DZ], state[:, r, h, 0:DZ],
                                                        power[:, 2 * P + 1:2 * P + 2], bank[f"kv{h}"][:, 0:DZ],
                                                        ALU.mult, ALU.add)
                    last.then_inc(s_state, 1)
                    dve.wait_ge(s_x1, n + 1)
                    stats(n, r, x1_sb[:, r, :], st2, mv2, s_st2, s_mv2, s_rs2)
                if it := att_item(k, u, SCORE):
                    n, g, r = it
                    dve.wait_ge(s_sc, n + 1)
                    need(dve, s_o, n - 1)
                    dve.tensor_tensor(att[:, r, :], bank["va"][:, D:D + P], decay[:], ALU.mult).then_inc(s_att, 1)
                if it := att_item(k, u, LOGIT):
                    n, g, r = it
                    dve.wait_ge(s_lg, n + 1)
                    dve.tensor_tensor(logits[:, bass.ds(n, 1), :].rearrange("p a e -> p (a e)"),
                                      bank["h"][:, D:D + NE], br_sb[:], ALU.add).then_inc(s_lgr, 1)
                if it := att_item(k, u, PROJ):
                    n, g, r = it
                    dve.wait_ge(s_vp, n + 1)
                    if isinstance(n, int) and n == 0:
                        dve.wait_ge(s_misc, 80)
                        dve.wait_ge(s_init, INIT)
                    need(dve, s_kv, n - 1)
                    dve.tensor_tensor(v_ext[:, r, 0:D], bank["va"][:, 0:D], bv_sb[:], ALU.add).then_inc(s_v, 1)
                first_stats(k, u)
                if isinstance(k, int) and (k, u) == (-1, 0):
                    mod_widths()
                    powers()
                if isinstance(k, int) and (k, u) == (0, 0):
                    mod_rows()

            slots(dve, *ATT, slot)

            hops = [0]

            def hop(ins):
                hops[0] += 1
                ins.then_inc(s_route, 1)
                dve.wait_ge(s_route, hops[0])

            scratch = arena[:, 0:9216]
            top = scratch[:, 0:NCH]
            hot = scratch[:, 64:64 + NCH * NE].rearrange("p (n e) -> p n e", e=NE)
            best = scratch[:, 320:320 + NCH]
            chosen = scratch[:, 384:640]
            chosen_ne = chosen.rearrange("p (e n) -> p n e", e=NE)
            chosen_en = chosen.rearrange("p (e n) -> p e n", e=NE)
            upto = scratch[:, 640:640 + NE * NCH + 1]
            count = scratch[:, 900:900 + NE]
            full = scratch[:, 908:908 + NE]
            upto_tile = scratch[:, 916:916 + NE]
            first = scratch[:, 924:924 + NE]
            over = scratch[:, 1024:1280].rearrange("p (e n) -> p e n", e=NE)
            place = scratch[:, 1280:1536]
            pos = scratch[:, 1536:1568]
            pos_i = scratch[:, 1568:1600].bitcast(I32)
            pos_tile = scratch[:, 1600:1632].bitcast(I32)
            pos_slot = scratch[:, 1632:1664].bitcast(I32)
            late = scratch[:, 1664:1664 + NT * NE].rearrange("p (t e) -> p t e", e=NE)
            tile_f = scratch[:, 1980:1980 + NT]
            token_f = scratch[:, 2020:2020 + NT]
            in_tile = scratch[:, 2048:2048 + NCH * NT].rearrange("p (n t) -> p n t", t=NT)
            in_slot = scratch[:, 3328:3328 + NCH * P].rearrange("p (n s) -> p n s", s=P)

            dve.wait_ge(s_lgr, NCH)
            for b in range(B):
                dve.wait_ge(s_sx[b], 16 * (NCH // B))
                dve.wait_ge(s_sh[b], 16 * (NCH // B))
            hop(dve.tensor_reduce(top, logits[:], AX_X, ALU.max))
            hop(dve.tensor_tensor(hot, logits[:], top.unsqueeze(2).to_broadcast([P, NCH, NE]), ALU.is_equal))
            hop(dve.tensor_tensor(hot, hot, con("weight8").unsqueeze(1).to_broadcast([P, NCH, NE]), ALU.mult))
            hop(dve.tensor_reduce(best, hot, AX_X, ALU.max))
            hop(dve.tensor_tensor(chosen_ne, hot, best.unsqueeze(2).to_broadcast([P, NCH, NE]), ALU.is_equal))
            dve.memset(upto[:, 0:1], 0.0).then_inc(s_chosen, 1)
            dve.wait_ge(s_rank, 1)
            ones256 = cst[:, 2 * P:2 * P + 1].to_broadcast([P, NE * NCH])
            hop(dve.tensor_tensor_scan(upto[:, 1:1 + NE * NCH], ones256, bank["va"][:, 0:NE * NCH], 0.0,
                                       ALU.mult, ALU.add))
            ends = upto[:, NCH:NE * NCH + 1:NCH]
            starts = upto[:, 0:NE * NCH:NCH]
            hop(dve.tensor_tensor(count, ends, starts, ALU.subtract))
            hop(dve.tensor_tensor(over, count.unsqueeze(2).to_broadcast([P, NE, NCH]),
                                  con("bounds").unsqueeze(1).to_broadcast([P, NE, NCH]), ALU.is_gt))
            hop(dve.tensor_reduce(full, over, AX_X, ALU.add))
            hop(dve.tensor_tensor_scan(upto_tile, cst[:, 2 * P:2 * P + 1].to_broadcast([P, NE]), full, 0.0,
                                       ALU.mult, ALU.add))
            hop(dve.tensor_tensor(first, upto_tile, full, ALU.subtract))
            hop(dve.scalar_tensor_tensor(first, first, float(P), starts, ALU.mult, ALU.subtract))
            hop(dve.tensor_tensor(place, bank["qk"][:, 0:NE * NCH], upto[:, 0:NE * NCH], ALU.add))
            place_en = place.rearrange("p (e n) -> p e n", e=NE)
            hop(dve.tensor_tensor(place_en, place_en, first.unsqueeze(2).to_broadcast([P, NE, NCH]), ALU.add))
            hop(dve.tensor_tensor(place, place, chosen, ALU.mult))
            hop(dve.tensor_reduce(pos, place.rearrange("p (e n) -> p n e", e=NE), AX_X, ALU.add))
            hop(dve.tensor_copy(pos_i, pos))
            hop(dve.tensor_scalar(pos_tile, pos_i, 7, None, ALU.arith_shift_right))
            hop(dve.tensor_scalar(pos_slot, pos_i, P - 1, None, ALU.bitwise_and))
            hop(dve.tensor_tensor(in_tile, pos_tile.unsqueeze(2).to_broadcast([P, NCH, NT]),
                                  con("tile_no").unsqueeze(1).to_broadcast([P, NCH, NT]), ALU.is_equal))
            hop(dve.tensor_tensor(in_tile, in_tile, con("token_less").unsqueeze(2).to_broadcast([P, NCH, NT]),
                                  ALU.mult))
            q = NCH // 4
            for i in range(4):
                dve.tensor_tensor(in_slot[:, i * q:(i + 1) * q, :],
                                  pos_slot[:, i * q:(i + 1) * q].unsqueeze(2).to_broadcast([P, q, P]),
                                  con("slot_no").unsqueeze(1).to_broadcast([P, q, P]),
                                  ALU.is_equal).then_inc(s_bits, 1)
            hop(dve.tensor_tensor(late[:, :, 0:NE - 1], con("tile_no").unsqueeze(2).to_broadcast([P, NT, NE - 1]),
                                  upto_tile[:, 0:NE - 1].unsqueeze(1).to_broadcast([P, NT, NE - 1]), ALU.is_ge))
            hop(dve.tensor_reduce(tile_f, late[:, :, 0:NE - 1], AX_X, ALU.add))
            hop(dve.tensor_copy(tile_expert[:], tile_f))
            dve.wait_ge(s_ids, 1)
            hop(dve.tensor_scalar(token_f, bank["x"][:, 0:NT], float(NTOK), None, ALU.add))
            hop(dve.tensor_copy(slot_token[:], token_f))
            hop(dve.tensor_scalar(slot_late[:], token_f, float(S), None, ALU.is_ge))
            dve.tensor_scalar(slot_early[:], token_f, float(S), None, ALU.is_lt).then_inc(s_routed, 1)

            dve.wait_ge(s_idx, 1)

            def slot(k, u):
                if it := ffn_item(k, u, 0):
                    n, g, r = it
                    dve.wait_ge(s_hp, 2 * n + 2)
                    need(dve, s_hx, 2 * n)
                    dve.tensor_copy(hid[:, 512:1024], bank["va"][:]).then_inc(s_hd, 1)
                if it := ffn_item(k, u, 1):
                    n, g, r = it
                    dve.wait_ge(s_y, n + 1)
                    need(dve, s_out[r], 16 * g)
                    dve.tensor_tensor(done_rows[:, r, :], bank["o"][:, 0:D], b2_now[:, r, :], ALU.add).then_inc(s_ys, 1)
                    dve.wait_ge(s_ys, 2 * n + 1)
                    dve.tensor_tensor(done_rows[:, r, :], done_rows[:, r, :], gate_now[:, r, :],
                                      ALU.mult).then_inc(s_ys, 1)
                    dve.wait_ge(s_ys, 2 * n + 2)
                    dve.tensor_tensor(done_rows[:, r, :], done_rows[:, r, :], tok[:, r, 0:D],
                                      ALU.add).then_inc(s_done, 1)
                if it := ffn_item(k, u, 0):
                    n, g, r = it
                    dve.wait_ge(s_hx, 2 * n + 2)
                    dve.wait_ge(s_prep, 5 * n + 5)
                    need(dve, s_y, n)
                    for f in range(FK // 2, FK):
                        last = dve.tensor_scalar(hid_t[:, f, :], bank["kv1"][:, (f - 4) * P:(f - 3) * P],
                                                 b1_now[:, r, f:f + 1], 0.0, ALU.add, ALU.max)
                    last.then_inc(s_htd, 1)

            slots(dve, *FFN, slot)

        @block.tensor
        def _(pe):
            pe.wait_ge(s_csilu, 1)
            pe.wait_ge(s_cmod, 32)
            for m in range(2 * DK):
                for k in range(DK):
                    last = pe.matmul(bank["k"][:, m * B:(m + 1) * B], wmod_sb[:, k, m * P:(m + 1) * P],
                                     c_silu[:, k, :], start=(k == 0), stop=(k == DK - 1))
            last.then_inc(s_modt, 1)

            def mod_rows():
                for b, names in enumerate((("kv0", "kv1"), ("o", "h"))):
                    for i, name in enumerate(names):
                        for k in range(DK):
                            last = pe.matmul(bank[name][:], c_wide[:, k, b, :],
                                             wmod_sb[:, k, (i + 1) * 512:(i + 2) * 512],
                                             start=(k == 0), stop=(k == DK - 1))
                    last.then_inc(s_modb, 1)

            def slot(k, u):
                if it := att_item(k, u, ATTEND):
                    n, g, r = it
                    if isinstance(n, int) and n == 0:
                        pe.wait_ge(s_init, INIT)
                        pe.wait_ge(s_modb_ready, B)
                    pe.wait_ge(s_att, n + 1)
                    pe.wait_ge(s_v, n + 1)
                    need(pe, s_x1, n)
                    pe.matmul(bank["o"][:, 0:DZ], att[:, r, :], v_ext[:, r, 0:DZ], start=True, stop=False)
                    pe.wait_ge(s_qg, n + 1)
                    need(pe, s_state, n - 1)
                    for h in range(DK):
                        last = pe.matmul(bank["o"][:, 0:DZ], qg_t[:, r, h, :], state[:, r, h, 0:DZ],
                                         start=False, stop=(h == DK - 1))
                    last.then_inc(s_o, 1)
                    pe.wait_ge(s_kg, n + 1)
                    need(pe, s_state, n)
                    for h in range(DK):
                        last = pe.matmul(bank[f"kv{h}"][:, 0:DZ], kg[:, r, h * P:(h + 1) * P], v_ext[:, r, 0:DZ],
                                         start=True, stop=True)
                    last.then_inc(s_kv, 1)
                if it := att_item(k, u, LOGIT):
                    n, g, r = it
                    pe.wait_ge(s_h2t, n + 1)
                    for h in range(DK):
                        last = pe.matmul(bank["h"][:, D:D + NE], h2_t[:, r, h, :], wr_sb[:, h, :],
                                         start=(h == 0), stop=(h == DK - 1))
                    last.then_inc(s_lg, 1)
                if it := att_item(k, u, SCORE):
                    n, g, r = it
                    pe.wait_ge(s_k, n + 1)
                    need(pe, s_kg, n)
                    for h in range(DK):
                        last = pe.transpose(bank["k"][:, h * P:(h + 1) * P], k_t[:, r, h, :], ident)
                    last.then_inc(s_kx, 1)
                    pe.wait_ge(s_v, n + 1)
                    for h in range(DK):
                        last = pe.matmul(bank["va"][:, D:D + P], k_t[:, r, h, :], q_t[:, r, h, :],
                                         start=(h == 0), stop=(h == DK - 1))
                    last.then_inc(s_sc, 1)
                if it := att_item(k, u, PROJ):
                    n, g, r = it
                    if isinstance(n, int) and n == 0:
                        pe.wait_ge(s_wqkv, 32)
                    pe.wait_ge(s_ht, n + 1)
                    need(pe, s_k, n)
                    for m in range(2):
                        for c in range(DK):
                            for h in range(DK):
                                last = pe.matmul(bank["qk"][:, (m * DK + c) * P:(m * DK + c + 1) * P],
                                                 wqkv_sb[:, m, h, c * P:(c + 1) * P], h_t[:, r, h, :],
                                                 start=(h == 0), stop=(h == DK - 1))
                    last.then_inc(s_qkp, 1)
                    need(pe, s_att, n)
                    for h in range(DK):
                        last = pe.matmul(bank["va"][:, 0:D], h_t[:, r, h, :], wqkv_sb[:, 2, h, :],
                                         start=(h == 0), stop=(h == DK - 1))
                    last.then_inc(s_vp, 1)
                if it := att_item(k, u, XPOSE2):
                    n, g, r = it
                    pe.wait_ge(s_h2, n + 1)
                    need(pe, s_h2t, n)
                    need(pe, s_lgr, n)
                    for h in range(DK):
                        last = pe.transpose(bank["h"][:, h * P:(h + 1) * P], h2[:, r, h * P:(h + 1) * P], ident)
                    last.then_inc(s_h2x, 1)
                if it := att_item(k, u, XPOSE):
                    n, g, r = it
                    if isinstance(n, int) and n == 0:
                        pe.wait_ge(s_const, 16)
                    pe.wait_ge(s_xn1, n + 1)
                    need(pe, s_ht, n)
                    for h in range(DK):
                        last = pe.transpose(bank["x"][:, h * P:(h + 1) * P], xn1[:, r, h * P:(h + 1) * P], ident)
                    last.then_inc(s_xt, 1)
                if isinstance(k, int) and (k, u) == (0, 0):
                    mod_rows()

            slots(pe, *ATT, slot)

            pe.wait_ge(s_chosen, 1)
            chosen = arena[:, 384:640]
            in_tile = arena[:, 2048:2048 + NCH * NT].rearrange("p (n t) -> p n t", t=NT)
            in_slot = arena[:, 3328:3328 + NCH * P].rearrange("p (n s) -> p n s", s=P)
            pe.matmul(bank["qk"][:, 0:NE * NCH], con("before"), chosen, start=True, stop=True)
            pe.matmul(bank["va"][:, 0:NE * NCH], con("ones"), chosen, start=True, stop=True).then_inc(s_rank, 1)
            for n in range(NCH):
                if n % (NCH // 4) == 0:
                    pe.wait_ge(s_bits, n // (NCH // 4) + 1)
                last = pe.matmul(bank["x"][:, 0:NT], in_slot[:, n, :], in_tile[:, n, :],
                                 start=(n == 0), stop=(n == NCH - 1))
            last.then_inc(s_ids, 1)

            pe.wait_ge(s_routed, 1)
            pe.wait_ge(s_experts, 16 * 2 * NE)
            pe.wait_ge(s_misc, 80)

            def slot(k, u):
                if it := ffn_item(k, u, 0):
                    n, g, r = it
                    e = pe.value_load(tile_expert[0:1, bass.ds(n, 1)], min_val=0, max_val=NE - 1)
                    pe.wait_ge(s_tt, n + 1)
                    for i, name in enumerate(("qk", "va")):
                        need(pe, (s_ha, s_hd)[i], n)
                        for h in range(DK):
                            last = pe.matmul(bank[name][:], tok_t[:, r, h, :],
                                             w1_sb[:, bass.ds(e, 1), h, i * 512:(i + 1) * 512].rearrange(
                                                 "p a f -> p (a f)"), start=(h == 0), stop=(h == DK - 1))
                        last.then_inc(s_hp, 1)
                if it := ffn_item(k, u, 1):
                    n, g, r = it
                    e = pe.value_load(tile_expert[0:1, bass.ds(n, 1)], min_val=0, max_val=NE - 1)
                    pe.wait_ge(s_hta, n + 1)
                    pe.wait_ge(s_htd, n + 1)
                    need(pe, s_done, n)
                    for f in range(FK):
                        last = pe.matmul(bank["o"][:, 0:D], hid_t[:, f, :],
                                         w2_sb[:, bass.ds(e, 1), f, :].rearrange("p a d -> p (a d)"),
                                         start=(f == 0), stop=(f == FK - 1))
                    last.then_inc(s_y, 1)
                if it := ffn_item(k, u, 0):
                    n, g, r = it
                    for i, name in enumerate(("kv0", "kv1")):
                        pe.wait_ge((s_ha, s_hd)[i], n + 1)
                        need(pe, (s_hta, s_htd)[i], n)
                        for f in range(4 * i, 4 * i + 4):
                            last = pe.transpose(bank[name][:, (f - 4 * i) * P:(f - 4 * i + 1) * P],
                                                hid[:, f * P:(f + 1) * P], ident)
                        last.then_inc(s_hx, 1)
                if it := ffn_item(k, u, -1):
                    n, g, r = it
                    pe.wait_ge(s_in[r], 16 * (g + 1))
                    need(pe, s_tt, n)
                    for h in range(DK):
                        last = pe.transpose(bank["h"][:, h * P:(h + 1) * P],
                                            tok[:, r, D + h * P:D + (h + 1) * P], ident)
                    last.then_inc(s_tx, 1)

            slots(pe, *FFN, slot)


def kernel(L0_attn_x_seq, L0_attn_Wq, L0_attn_bq, L0_attn_Wk, L0_attn_bk, L0_attn_Wv, L0_attn_bv, L0_attn_gamma,
           L0_ffn_Wr, L0_ffn_br, L0_ffn_W1, L0_ffn_b1, L0_ffn_W2, L0_ffn_b2, L0_c, L0_wmod):
    import concourse.bacc as bacc
    from concourse.bass_utils import run_bass_kernel_spmd

    def by_width(a):
        a = np.asarray(a)
        return np.moveaxis(a.reshape(*a.shape[:-1], -1, P), -1, 0)

    def rows_of(a, shape):
        return np.broadcast_to(np.asarray(a).reshape(1, -1), (P, int(np.prod(shape)))).reshape(P, *shape)

    qkv = np.stack([np.asarray(w) for w in (L0_attn_Wq, L0_attn_Wk, L0_attn_Wv)])
    consts, exps = constants()
    laid = {
        "x": np.asarray(L0_attn_x_seq).reshape(NTOK, D),
        "wqkv": by_width(qkv).transpose(0, 1, 3, 2),
        "bqk": by_width(np.stack([np.asarray(L0_attn_bq), np.asarray(L0_attn_bk)])),
        "bvb": rows_of(L0_attn_bv, (D,)),
        "gamma": rows_of(L0_attn_gamma, (1,)),
        "wr": by_width(L0_ffn_Wr).transpose(0, 2, 1),
        "brb": rows_of(L0_ffn_br, (NE,)),
        "w1": by_width(L0_ffn_W1).transpose(1, 0, 3, 2),
        "b1": by_width(L0_ffn_b1),
        "w2": by_width(L0_ffn_W2).transpose(1, 0, 3, 2),
        "b2b": rows_of(L0_ffn_b2, (NE, D)),
        "c_t": by_width(L0_c).transpose(0, 2, 1),
        "wmod": np.asarray(L0_wmod).reshape(DK, P, 6 * D).transpose(1, 0, 2),
        "consts": consts,
        "exps": exps,
    }
    nc = bacc.Bacc("TRN2", target_bir_lowering=False, num_devices=1)
    arrays, args = {}, []
    for name, a in laid.items():
        a = np.ascontiguousarray(a)
        arrays[f"in_{name}"] = a
        args.append(nc.dram_tensor(f"in_{name}", a.shape, mybir.dt.from_np(a.dtype), kind="ExternalInput").ap())
    args.append(nc.dram_tensor("out_rows", (NTOK, D), F32, kind="ExternalOutput").ap())
    build(nc, *args)
    r = run_bass_kernel_spmd(nc, [arrays], core_ids=[0])
    return r.results[0]["out_rows"].reshape(B, S, D)
```

```python
from contextlib import ExitStack

import numpy as np

import concourse.bass as bass
from concourse import mybir

F32 = mybir.dt.float32
F16 = mybir.dt.float16
I32 = mybir.dt.int32
ALU = mybir.AluOpType
ACT = mybir.ActivationFunctionType
AX_X, AX_XY = mybir.AxisListType.X, mybir.AxisListType.XY

P = 128
B, S, D = 2, 2048, 256
DK = D // P
NE, F = 8, 1024
FK = F // P
NTOK = B * S
NCH = NTOK // P
NT = NCH + NE - 1
DZ = D + 1
LN_EPS, DEN_EPS = 1e-5, 1e-6
INIT = B * (DK + 1) + 3

LOAD, STATS, NORM, XPOSE, PROJ, SCORE, ATTEND, NORM2, XPOSE2, LOGIT = -6, -3, -2, -1, 0, 1, 2, 3, 4, 5
COLS = {}
_at = 0
for _name, _n in (("ident", P), ("before", P), ("ones", P), ("slot_no", P), ("tile_no", NT), ("weight8", NE),
                  ("bounds", NCH), ("chunk_less", NCH), ("lane", 1)):
    COLS[_name] = (_at, _at + _n)
    _at += _n
NCONST = _at
NM = 2 * NE
MW = DK * F
TOP = 14
EXPONENT = 0x7F800000
EXP_ONE = 1 << 23
HID_SCALE = 2.0 ** -23


def constants():
    p = np.arange(P)
    c = np.zeros((P, NCONST), np.float32)

    def put(name, value):
        a, b = COLS[name]
        c[:, a:b] = value

    put("ident", np.eye(P))
    put("before", p[:, None] < p[None, :])
    put("ones", 1.0)
    put("slot_no", p[None, :])
    put("tile_no", np.arange(NT)[None, :])
    put("weight8", NE - np.arange(NE)[None, :])
    put("bounds", (P * np.arange(NCH))[None, :])
    n = np.arange(NCH)
    put("chunk_less", ((n % B) * (S // P) + n // B - NTOK // P)[None, :])
    put("lane", p[:, None])
    return c


def need(eng, sem, count):
    if isinstance(count, int) and count <= 0:
        return
    eng.wait_ge(sem, count)


def slots(eng, unroll, first, loop, last, slot):
    for k in range(first, loop[0]):
        for u in range(unroll):
            slot(k, u)
    if loop[1] > loop[0]:
        with eng.Fori(loop[0], loop[1], 1) as k:
            for u in range(unroll):
                slot(k, u)
    for k in range(loop[1], last + 1):
        for u in range(unroll):
            slot(k, u)


def item(k, u, lag, unroll, count):
    q, r = divmod(u - lag, unroll)
    g = k + q
    n = g * unroll + r
    if isinstance(n, int) and not 0 <= n < count:
        return None
    return n, g, r


ATT = (B, -3, (4, 13), 18)
ATT_S = (B, -3, (4, 4), 18)
FFN = (4, -1, (2, 9), 9)
MAX, HI, LO = 0, 1, 2
PIECES, STAGES = 4, 4


def build(nc, x, wqkv, bqk, bvb, gamma, wr, brb, w_raw, b1, b2b, c_t, wmod, consts, out):
    rows = nc.dram_tensor("token_rows", [NTOK, 2 * D], F32, kind="Internal").ap()
    mods = nc.dram_tensor("mod_rows", [1, B * 4 * D], F32, kind="Internal").ap()
    with ExitStack() as ctx:
        def sb(name, shape, dt=F32):
            return ctx.enter_context(nc.sbuf_tensor(name, shape, dt))

        def sem(name):
            return ctx.enter_context(nc.semaphore(name))

        bank = {n: ctx.enter_context(nc.psum_tensor(f"ps_{n}", [P, 512], F32))
                for n in ("o", "kv0", "kv1", "qk", "va", "x", "h", "k")}

        w = sb("w", [P, NM + 1, 2, MW], F16)
        w_scale = sb("w_scale", [P, NM])
        w_unscale = sb("w_unscale", [P, NM])
        w_floor = sb("w_floor", [P, NM])
        cst = sb("cst", [P, NCONST])
        wqkv_sb = sb("wqkv_sb", [P, 3, DK, D])
        bqk_sb = sb("bqk_sb", [P, 2, DK])
        bv_sb = sb("bv_sb", [P, D])
        wr_sb = sb("wr_sb", [P, DK, NE])
        br_sb = sb("br_sb", [P, NE])
        b1_sb = sb("b1_sb", [P, NE, FK])
        b2_sb = sb("b2_sb", [P, NE, D])
        mod_t = sb("mod_t", [P, 2 * DK, B])
        mod_rows_sb = sb("mod_rows_sb", [P, B, 4, D])
        gate_a, shift_b, scale_b, gate_b = (mod_rows_sb[:, :, i, :] for i in range(4))
        logits = sb("logits", [P, NCH, NE])
        power = sb("power", [P, P])
        decay = sb("decay", [P, P])
        slot_token = sb("slot_token", [P, NT], I32)
        slot_late = sb("slot_late", [P, NT])
        slot_early = sb("slot_early", [P, NT])
        tile_matrix = sb("tile_matrix", [P, NT], I32)

        arena = sb("arena", [P, 9216])
        at = [0]

        def cut(*shape):
            n = int(np.prod(shape))
            v = arena[:, at[0]:at[0] + n]
            at[0] += n
            assert at[0] <= 9216, at
            if len(shape) == 2:
                v = v.rearrange("p (a b) -> p a b", a=shape[0])
            if len(shape) == 3:
                v = v.rearrange("p (a b c) -> p a b c", a=shape[0], b=shape[1])
            return v

        x_sb = cut(B, 4, D)
        xn1 = cut(B, D)
        h_t = cut(B, DK, P)
        q_t = cut(B, DK, P)
        k_t = cut(B, DK, P)
        qg_t = cut(B, DK, P)
        kg = cut(B, D)
        v_ext = cut(B, DZ + 1)
        att = cut(B, P)
        x1_sb = cut(B, D)
        xn2 = cut(B, D)
        h2 = cut(B, D)
        h2_t = cut(B, DK, P)
        state = cut(B, DK, DZ + 1)
        small = sb("small", [P, 64])
        st1, st2 = sb("st1", [P, B, 6]), sb("st2", [P, B, 6])
        mv1, mv2 = sb("mv1", [P, B, 2]), sb("mv2", [P, B, 2])
        rs1, rs2 = sb("rs1", [P, B, 4]), sb("rs2", [P, B, 4])
        den = sb("den", [P, B, 2])
        attended = sb("attended", [P, B, D])
        att_end = at[0]

        at[0] = 0
        tok = cut(4, 2 * D)
        hid = cut(FK, P)
        done_rows = cut(2, D)
        gate_now = cut(4, D)
        gate_part = cut(2, 2, D)
        tok_s = cut(2, DK * P)
        hid_s = cut(2, FK * P)
        b1_now = cut(4, FK)
        assert at[0] <= 9216
        idx_in = sb("idx_in", [P, 4], I32)
        idx_out = sb("idx_out", [P, 2], I32)

        tok_parts = tok_s.bitcast(F16).rearrange("p r (i k t) -> p r i k t", i=2, k=DK)
        hid_parts = hid_s.bitcast(F16).rearrange("p r (i f t) -> p r i f t", i=2, f=FK)
        w1_now = w[:, NM]
        scale_now = sb("scale_now", [P, 4, 2])

        spare = w[:, 10:13].rearrange("p m i c -> p (m i c)").bitcast(F32)
        wmod_sb = spare[:, 0:DK * 6 * D].rearrange("p (k m) -> p k m", k=DK)
        _o = DK * 6 * D
        c_sb = spare[:, _o:_o + 4].rearrange("p (k b) -> p k b", k=DK)
        c_exp = spare[:, _o + 4:_o + 8].rearrange("p (k b) -> p k b", k=DK)
        c_silu = spare[:, _o + 8:_o + 12].rearrange("p (k b) -> p k b", k=DK)
        sign_sb = spare[0:B, _o + 16:_o + 16 + D]
        mag_sb = spare[0:B, _o + 16 + D:_o + 16 + 2 * D]
        raw_sb = spare[0:B, _o + 16 + 2 * D:_o + 16 + 3 * D]
        mod2_sb = spare[0:B, _o + 16 + 3 * D:_o + 16 + 7 * D]
        raw_w = w[:].rearrange("p m i c -> p m (i c)").bitcast(F32)
        gamma_sb, fixed = small[:, 0:1], small[:, 8:11]
        x_scale, x_unscale = small[:, 12:13], small[:, 13:14]
        b1_max, b1_all = small[:, 16:16 + NE], small[:, 24:24 + NE]
        piece_max, w_most, all_max = small[:, 52:52 + PIECES], small[:, 34:35], small[:, 35:36]
        bits, x_most = small[:, 36:37], small[:, 40:44]
        hid_unit, y_unit = small[:, 44:45], small[:, 45:46]
        c16 = sb("c16", [P, 3 * P + NT], F16)
        before16, ones16 = c16[:, 0:P], c16[:, P:2 * P]
        slot_no16, tile_no16 = c16[:, 2 * P:3 * P], c16[:, 3 * P:3 * P + NT]

        def con(name):
            a, b = COLS[name]
            return cst[:, a:b]

        ident = con("ident")

        s_const, s_x = sem("constants_landed"), [sem(f"x_landed_{b}") for b in range(B)]
        s_cmod, s_gamma, s_wqkv, s_misc = (sem("c_wmod_landed"), sem("gamma_landed"), sem("wqkv_landed"),
                                           sem("biases_landed"))
        s_wraw, s_c = sem("w_raw_landed"), sem("c_landed")
        (s_wmaxh, s_wboth, s_wmax, s_wbits, s_wscale, s_whi, s_wlo) = map(sem, (
            "w_max_halves", "w_max_lane", "w_max_all", "w_scale_step", "w_scale_ready", "w_hi_ready", "w_lo_ready"))
        s_ready = sem("tile_constants_all_ready")
        s_w1 = sem("w1_half_copied")
        s_gpart, s_gate = sem("gate_part_ready"), sem("gate_ready")
        s_modd, s_modl, s_bound, s_bmax, s_xstep, s_xscale, s_c16, s_hhi, s_hlo, s_thi, s_tlo = map(sem, (
            "mod_rows_in_dram", "mod_rows_landed", "b1_max_lane", "b1_max_all", "x_scale_step", "x_scale_ready",
            "consts16_ready", "hid_hi_ready", "hid_lo_ready", "tok_hi_ready", "tok_lo_ready"))
        s_cexp, s_csilu, s_modt, s_modt_ready = (sem("c_exp_ready"), sem("c_silu_ready"), sem("mod_t_done"),
                                                 sem("mod_t_ready"))
        s_modb, s_modb_ready, s_setup = sem("mod_rows_done"), sem("mod_rows_ready"), sem("setup_step")
        s_pow = sem("power_step")
        s_marks = sem("marks")
        s_decay, s_init = sem("decay_ready"), sem("state_cleared")
        (s_st1, s_mv1, s_rs1s, s_rs1, s_xn1, s_xt, s_ht) = map(sem, (
            "stats1", "mean_var1", "rstd1_step", "rstd1", "xn1_ready", "x_transposed", "h_t_ready"))
        (s_qkp, s_vp, s_q, s_k, s_qg, s_v) = map(sem, (
            "qk_projected", "v_projected", "q_ready", "k_ready", "qg_ready", "v_ready"))
        (s_kx, s_kg, s_sc, s_att) = map(sem, ("k_transposed", "kg_ready", "scores_done", "att_ready"))
        (s_o, s_kv, s_state, s_den, s_rden, s_atn, s_x1) = map(sem, (
            "attended_done", "kv_done", "state_ready", "den_ready", "rden_ready", "attended_ready", "x1_ready"))
        (s_st2, s_mv2, s_rs2s, s_rs2, s_xn2, s_h2s, s_h2) = map(sem, (
            "stats2", "mean_var2", "rstd2_step", "rstd2", "xn2_ready", "h2_step", "h2_ready"))
        (s_h2x, s_h2t, s_lg, s_lgr) = map(sem, ("h2_transposed", "h2_t_ready", "logits_done", "logits_ready"))
        s_sx = [sem(f"x1_stored_{b}") for b in range(B)]
        s_sh = [sem(f"h2_stored_{b}") for b in range(B)]
        s_route, s_chosen, s_rank, s_bits, s_ids, s_routed = map(sem, (
            "route_step", "chosen_ready", "ranks_done", "slots_hot", "ids_done", "routed"))
        s_in = [sem(f"tokens_gathered_{r}") for r in range(4)]
        s_out = [sem(f"rows_scattered_{r}") for r in range(2)]
        (s_idx, s_prep, s_preps, s_tx, s_tt, s_hp, s_ha, s_hd, s_hx, s_hta, s_htd, s_y, s_ys, s_done) = map(sem, (
            "index_copied", "tile_constants_ready", "tile_constants_step", "tokens_transposed", "tok_t_ready",
            "hidden_done", "hidden_ready_act", "hidden_ready_dve", "hidden_transposed", "hid_t_ready_act",
            "hid_t_ready_dve", "y_done", "y_step", "rows_done"))

        scratch = arena[:, 4 * 2 * D:9216]
        chosen16 = scratch[:, 384:512].bitcast(F16)
        in_tile = scratch[:, 2112:2112 + NCH * NT].bitcast(F16).rearrange("p (n i t) -> p n i t", i=2, t=NT)
        hot_tile = scratch[:, 3392:3392 + NCH * NT // 2].bitcast(F16).rearrange("p (n t) -> p n t", t=NT)
        in_slot = scratch[:, 4096:4096 + NCH * P // 2].bitcast(F16).rearrange("p (n s) -> p n s", s=P)

        block = ctx.enter_context(nc.Block())

        def att_item(k, u, lag):
            return item(k, u, lag, B, NCH)

        def ffn_item(k, u, lag):
            return item(k, u, lag, FFN[0], NT)

        def alone(eng, *waits):
            for w, c in waits:
                need(eng, w, c)
                eng.sem_inc(s_marks, 1)

        def matrix_at(k, lag):
            m = k - lag
            return m if not isinstance(m, int) or 0 <= m < NM else None

        def landing(m):
            return (m + STAGES - 1 - (NM - 1) % STAGES) % STAGES + NM + 1 - STAGES

        def piece(v, i):
            return v[:, i * (MW // PIECES):(i + 1) * (MW // PIECES)]

        def raw_piece(m, i):
            return piece(raw_w[:, bass.ds(landing(m), 1), :].rearrange("p a c -> p (a c)"), i)

        def part_piece(m, part, i):
            return piece(w[:, bass.ds(m, 1), part, :].rearrange("p a c -> p (a c)"), i)

        def load_matrix(eng, m):
            alone(eng, (s_wraw, 16 * m), (s_wlo, m - STAGES + 1))
            eng.dma_start(raw_w[:, bass.ds(landing(m), 1), :].rearrange("p a c -> p (a c)"),
                          w_raw[bass.ds(m, 1)].rearrange("a p c -> p (a c)")).then_inc(s_wraw, 16)

        def token_row(g, r):
            return r * S + g * P

        @block.sync
        def _(sp):
            sp.dma_start(c_sb, c_t).then_inc(s_c, 16)

            def slot(k, u):
                if it := att_item(k, u, LOAD):
                    n, g, r = it
                    alone(sp, (s_x[r], g * 16), (s_x1, n - 7))
                    sp.dma_start(x_sb[:, r, bass.ds(g % 4, 1), :].rearrange("p a d -> p (a d)"),
                                 x[bass.ds(token_row(g, r), P), :]).then_inc(s_x[r], 16)
                    if isinstance(n, int) and n == 0:
                        sp.dma_start(cst[:], consts).then_inc(s_const, 16)
                    if isinstance(n, int) and n == 1:
                        sp.dma_start(wqkv_sb[:], wqkv).then_inc(s_wqkv, 16)
                        sp.dma_start(bqk_sb[:], bqk).then_inc(s_wqkv, 16)
                        sp.dma_start(bv_sb[:], bvb).then_inc(s_misc, 16)
                        sp.dma_start(wr_sb[:], wr).then_inc(s_misc, 16)
                        sp.dma_start(br_sb[:], brb).then_inc(s_misc, 16)
                        sp.dma_start(b1_sb[:], b1).then_inc(s_misc, 16)
                        sp.dma_start(b2_sb[:], b2b).then_inc(s_misc, 16)
                if it := att_item(k, u, ATTEND):
                    n, g, r = it
                    alone(sp, (s_sx[r], g * 16), (s_x1, n + 1))
                    sp.dma_start(rows[bass.ds(token_row(g, r), P), 0:D], x1_sb[:, r, :]).then_inc(s_sx[r], 16)
                if isinstance(k, int) and (k, u) == (0, 0):
                    sp.wait_ge(s_modb_ready, 1)
                    sp.dma_start(mods.rearrange("a (b m) -> (a b) m", b=B), mod2_sb).then_inc(s_modd, 16)
                    sp.wait_ge(s_modd, 16)
                    sp.dma_start(mod_rows_sb[:].rearrange("p b m d -> p (b m d)"),
                                 mods.to_broadcast([P, B * 4 * D])).then_inc(s_modl, 16)
                if it := att_item(k, u, NORM2):
                    n, g, r = it
                    alone(sp, (s_sh[r], g * 16), (s_h2, n + 1))
                    sp.dma_start(rows[bass.ds(token_row(g, r), P), D:2 * D], h2[:, r, :]).then_inc(s_sh[r], 16)
                if u == 1 and isinstance(k, int) and -2 <= k < STAGES - 2:
                    load_matrix(sp, k + 2)
                if u == 1 and (not isinstance(k, int) or STAGES - 1 <= k < NM - 1):
                    load_matrix(sp, k + 1)

            slots(sp, *ATT, slot)

        @block.gpsimd
        def _(pool):
            for b in range(B):
                for k in range(DK):
                    pool.memset(state[:, b, k, :], 0.0).then_inc(s_init, 1)
                pool.memset(v_ext[:, b, D:DZ], 1.0).then_inc(s_init, 1)

            def inverse_deviation(n, r, s_mv, mv, rs, s_step, s_free, s_ready):
                pool.wait_ge(s_mv, n + 1)
                need(pool, s_free, n - 1)
                pool.tensor_tensor(rs[:, r, 0:1], mv[:, r, 1:2], fixed[:, 1:2], ALU.add).then_inc(s_step, 1)
                pool.wait_ge(s_step, 3 * n + 1)
                pool.tensor_tensor(rs[:, r, 1:2], rs[:, r, 0:1], fixed[:, 0:1], ALU.pow).then_inc(s_step, 1)
                pool.wait_ge(s_step, 3 * n + 2)
                pool.tensor_tensor(rs[:, r, 3:4], mv[:, r, 0:1], rs[:, r, 1:2], ALU.mult).then_inc(s_step, 1)
                pool.wait_ge(s_step, 3 * n + 3)
                pool.tensor_tensor(rs[:, r, 2:3], rs[:, r, 3:4], fixed[:, 2:3], ALU.mult).then_inc(s_ready, 1)

            for i, value in enumerate((-0.5, LN_EPS, -1.0)):
                pool.memset(fixed[:, i:i + 1], value).then_inc(s_init, 1)
            pool.wait_ge(s_init, INIT)

            def slot(k, u):
                if isinstance(k, int) and (k, u) == (-1, 1):
                    pool.wait_ge(s_bound, 1)
                    pool.partition_all_reduce(b1_all, b1_max, P, bass.bass_isa.ReduceOp.max).then_inc(s_bmax, 1)
                if it := att_item(k, u, NORM):
                    n, g, r = it
                    inverse_deviation(n, r, s_mv1, mv1, rs1, s_rs1s, s_xn1, s_rs1)
                if it := att_item(k, u, NORM2):
                    n, g, r = it
                    inverse_deviation(n, r, s_mv2, mv2, rs2, s_rs2s, s_xn2, s_rs2)
                    if isinstance(n, int) and n == 0:
                        pool.wait_ge(s_modl, 16)
                    pool.wait_ge(s_xn2, n + 1)
                    need(pool, s_h2x, n - 1)
                    need(pool, s_sh[r], 16 * g)
                    pool.tensor_tensor(xn2[:, r, :], xn2[:, r, :], scale_b[:, r, :], ALU.mult).then_inc(s_h2s, 1)
                    pool.wait_ge(s_h2s, n + 1)
                    pool.tensor_tensor(h2[:, r, :], xn2[:, r, :], shift_b[:, r, :], ALU.add).then_inc(s_h2, 1)
                if u == 0 and (m := matrix_at(k, MAX + 1)) is not None:
                    alone(pool, (s_wboth, m + 1))
                    pool.partition_all_reduce(all_max, w_most, P, bass.bass_isa.ReduceOp.max).then_inc(s_wmax, 1)
                if it := att_item(k, u, PROJ):
                    n, g, r = it
                    if isinstance(n, int) and n == 0:
                        pool.wait_ge(s_decay, 1)
                    pool.wait_ge(s_q, n + 1)
                    need(pool, s_o, n - 1)
                    pool.tensor_tensor(qg_t[:, r], q_t[:, r],
                                       power[:].unsqueeze(1).to_broadcast([P, DK, P]),
                                       ALU.mult).then_inc(s_qg, 1)

            slots(pool, *ATT, slot)

            for b in range(B):
                pool.wait_ge(s_sx[b], 16 * (NCH // B))
                pool.wait_ge(s_sh[b], 16 * (NCH // B))
            pool.wait_ge(s_x1, NCH)
            pool.memset(tok, 0.0).then_inc(s_idx, 1)
            pool.wait_ge(s_idx, 1)
            pool.wait_ge(s_routed, 1)

            def slot(k, u):
                if it := ffn_item(k, u, -1):
                    n, g, r = it
                    pool.wait_ge(s_gpart, n + 1)
                    need(pool, s_done, n - 3)
                    pool.tensor_tensor(gate_now[:, r, :], gate_part[:, r % 2, 0, :], gate_part[:, r % 2, 1, :],
                                       ALU.add).then_inc(s_gate, 1)
                if it := ffn_item(k, u, 1):
                    n, g, r = it
                    landed = 16 * (2 * g + r // 2)
                    need(pool, s_out[r % 2], landed)
                    pool.tensor_copy(idx_out[:, r % 2:r % 2 + 1], slot_token[:, bass.ds(n, 1)]).then_inc(s_preps, 1)
                    pool.wait_ge(s_ys, 2 * n + 2)
                    pool.tensor_tensor(done_rows[:, r % 2, :], done_rows[:, r % 2, :], tok[:, r, 0:D],
                                       ALU.add).then_inc(s_done, 1)
                    alone(pool, (s_preps, n + 1), (s_done, n + 1))
                    pool.indirect_dma_start(out, bass.IndirectOffsetOnAxis(idx_out[:, r % 2:r % 2 + 1], 0),
                                            done_rows[:, r % 2, :], None, bounds_check=NTOK - 1,
                                            oob_is_err=False).then_inc(s_out[r % 2], 16)
                if it := ffn_item(k, u, -3):
                    n, g, r = it
                    need(pool, s_done, n - 3)
                    pool.tensor_copy(idx_in[:, r:r + 1], slot_token[:, bass.ds(n, 1)]).then_inc(s_idx, 1)
                    alone(pool, (s_idx, n + 2), (s_in[r], 16 * g))
                    pool.indirect_dma_start(tok[:, r, :], None, rows,
                                            bass.IndirectOffsetOnAxis(idx_in[:, r:r + 1], 0),
                                            bounds_check=NTOK - 1, oob_is_err=False).then_inc(s_in[r], 16)
                    m = pool.value_load(tile_matrix[0:1, bass.ds(n, 1)], min_val=0, max_val=NM - 2)
                    b1_of = b1_sb[:].rearrange("p e (a f) -> p (e a) f", a=2)[:, bass.ds(m, 2), :]
                    pool.tensor_tensor(b1_now[:, r, :], b1_of.rearrange("p a f -> p (a f)"),
                                       w_scale[:, bass.ds(m, 1)].to_broadcast([P, FK]), ALU.mult).then_inc(s_prep, 1)
                    pool.tensor_tensor(scale_now[:, r, 0:1], w_unscale[:, bass.ds(m, 1)],
                                       w_unscale[:, bass.ds(m + 1, 1)], ALU.mult).then_inc(s_prep, 1)
                    pool.wait_ge(s_prep, 2 * n + 2)
                    pool.tensor_tensor(b1_now[:, r, :], b1_now[:, r, :], hid_unit.to_broadcast([P, FK]), ALU.mult)
                    pool.tensor_tensor(scale_now[:, r, 1:2], scale_now[:, r, 0:1], y_unit,
                                       ALU.mult).then_inc(s_ready, 1)

            slots(pool, *FFN, slot)
            for r in range(2):
                pool.wait_ge(s_out[r], 16 * ((NT + 1 - r) // 2))

        @block.scalar
        def _(act):
            act.dma_start(gamma_sb, gamma).then_inc(s_gamma, 16)
            act.dma_start(wmod_sb, wmod).then_inc(s_cmod, 16)
            act.wait_ge(s_c, 16)
            act.activation(c_exp, c_sb, ACT.Exp, scale=-1.0).then_inc(s_cexp, 1)
            def hi_piece(k, u, j):
                if (m := matrix_at(k, HI + 1 - u)) is not None:
                    i = 2 * (1 - u) + j
                    if i == 0:
                        act.wait_ge(s_wscale, m + 1)
                        if isinstance(m, int) and m > NM - STAGES:
                            act.wait_ge(s_wlo, m)
                    act.activation(part_piece(m, 0, i), raw_piece(m, i), ACT.Copy,
                                   scale=w_scale[:, bass.ds(m, 1)]).then_inc(s_whi, 1)

            def slot(k, u):
                if it := att_item(k, u, SCORE):
                    n, g, r = it
                    act.wait_ge(s_kx, n + 1)
                    need(act, s_kv, n - 1)
                    act.activation(kg[:, r, :], bank["k"][:, 0:D], ACT.Copy,
                                   scale=decay[:, P - 1:P]).then_inc(s_kg, 1)
                hi_piece(k, u, 0)
                if it := att_item(k, u, NORM2):
                    n, g, r = it
                    act.wait_ge(s_rs2, n + 1)
                    need(act, s_h2, n - 1)
                    act.activation(xn2[:, r, :], x1_sb[:, r, :], ACT.Identity, bias=rs2[:, r, 2:3],
                                   scale=rs2[:, r, 1:2]).then_inc(s_xn2, 1)
                if it := att_item(k, u, PROJ):
                    n, g, r = it
                    act.wait_ge(s_qkp, n + 1)
                    need(act, s_sc, n - 1)
                    need(act, s_qg, n - 1)
                    for h in range(DK):
                        last = act.activation(q_t[:, r, h, :], bank["qk"][:, h * P:(h + 1) * P], ACT.Relu,
                                              bias=bqk_sb[:, 0, h:h + 1])
                    last.then_inc(s_q, 1)
                    for h in range(DK):
                        last = act.activation(k_t[:, r, h, :], bank["qk"][:, D + h * P:D + (h + 1) * P], ACT.Relu,
                                              bias=bqk_sb[:, 1, h:h + 1])
                    last.then_inc(s_k, 1)
                if it := att_item(k, u, XPOSE2):
                    n, g, r = it
                    act.wait_ge(s_h2x, n + 1)
                    need(act, s_lg, n - 1)
                    act.activation(h2_t[:, r], bank["h"][:, 0:D].rearrange("p (k t) -> p k t", k=DK),
                                   ACT.Copy).then_inc(s_h2t, 1)
                if it := att_item(k, u, XPOSE):
                    n, g, r = it
                    act.wait_ge(s_xt, n + 1)
                    if isinstance(n, int) and n == 0:
                        act.wait_ge(s_modt_ready, 1)
                    need(act, s_vp, n - 1)
                    for h in range(DK):
                        last = act.activation(h_t[:, r, h, :], bank["x"][:, h * P:(h + 1) * P], ACT.Identity,
                                              bias=mod_t[:, h, r:r + 1], scale=mod_t[:, DK + h, r:r + 1])
                    last.then_inc(s_ht, 1)
                if it := att_item(k, u, NORM):
                    n, g, r = it
                    act.wait_ge(s_rs1, n + 1)
                    need(act, s_xt, n - 1)
                    act.activation(xn1[:, r, :], x_sb[:, r, bass.ds(g % 4, 1), :].rearrange("p a d -> p (a d)"),
                                   ACT.Identity, bias=rs1[:, r, 2:3], scale=rs1[:, r, 1:2]).then_inc(s_xn1, 1)
                hi_piece(k, u, 1)

            slots(act, *ATT, slot)

            act.wait_ge(s_idx, 1)

            def hidden(n, r, h):
                act.wait_ge(s_hp, 2 * n + h + 1)
                act.wait_ge(s_ready, n + 1)
                need(act, s_hlo, 2 * n + h - 1)
                for f in range(4 * h, 4 * h + 4):
                    last = act.activation(hid[:, f, :], bank[("qk", "va")[h]][:, (f % 4) * P:(f % 4 + 1) * P],
                                          ACT.Relu, bias=b1_now[:, r, f:f + 1], scale=HID_SCALE)
                last.then_inc(s_ha, 1)

            def hidden_hi(n, r, h):
                act.wait_ge(s_ha, 2 * n + h + 1)
                need(act, s_y, n - 1)
                act.activation(hid_parts[:, r % 2, 0, 4 * h:4 * h + 4, :], hid[:, 4 * h:4 * h + 4, :],
                               ACT.Copy).then_inc(s_hhi, 1)

            def slot(k, u):
                if it := ffn_item(k, u, -1):
                    n, g, r = it
                    if isinstance(n, int) and n == 0:
                        act.wait_ge(s_routed, 1)
                    need(act, s_gate, n - 1)
                    act.activation(gate_part[:, r % 2, 0, :], gate_b[:, 0, :], ACT.Copy,
                                   scale=slot_early[:, bass.ds(n, 1)])
                    act.activation(gate_part[:, r % 2, 1, :], gate_b[:, 1, :], ACT.Copy,
                                   scale=slot_late[:, bass.ds(n, 1)]).then_inc(s_gpart, 1)
                if it := ffn_item(k, u, 0):
                    hidden(it[0], it[2], 0)
                    hidden_hi(it[0], it[2], 0)
                if it := ffn_item(k, u, -1):
                    n, g, r = it
                    act.wait_ge(s_tx, n + 1)
                    need(act, s_hp, 2 * (n - 1))
                    act.activation(tok_parts[:, r % 2, 0], bank["h"][:, 0:D].rearrange("p (k t) -> p k t", k=DK),
                                   ACT.Copy, scale=x_scale).then_inc(s_thi, 1)
                if it := ffn_item(k, u, 0):
                    hidden(it[0], it[2], 1)
                    hidden_hi(it[0], it[2], 1)

            slots(act, *FFN, slot)

        @block.vector
        def _(dve):
            steps = [0]

            def step(ins):
                steps[0] += 1
                ins.then_inc(s_setup, 1)
                dve.wait_ge(s_setup, steps[0])

            dve.wait_ge(s_cexp, 1)
            step(dve.tensor_scalar(c_exp, c_exp, 1.0, None, ALU.add))
            step(dve.reciprocal(c_exp, c_exp))
            step(dve.tensor_tensor(c_silu, c_sb, c_exp, ALU.mult))
            dve.memset(small[:, 50:51], 0.0).then_inc(s_csilu, 1)
            dve.wait_ge(s_const, 16)
            dve.wait_ge(s_gamma, 16)
            step(dve.tensor_tensor_scan(decay[:], gamma_sb.to_broadcast([P, P]), con("ident"), 0.0, ALU.mult, ALU.add))
            dve.tensor_tensor_scan(power[:], gamma_sb.to_broadcast([P, P]), con("ones"), 1.0,
                                   ALU.mult, ALU.mult).then_inc(s_decay, 1)
            dve.wait_ge(s_decay, 1)

            def first_stats(k, u):
                if it := att_item(k, u, STATS):
                    n, g, r = it
                    dve.wait_ge(s_x[r], 16 * (g + 1))
                    dve.bn_stats(st1[:, r, :], x_sb[:, r, g % 4, :]).then_inc(s_st1, 1)

            def first_mean_var(k, u):
                if it := att_item(k, u, STATS):
                    n, g, r = it
                    need(dve, s_rs1, n - 1)
                    dve.wait_ge(s_st1, n + 1)
                    dve.bn_aggr(mv1[:, r, :], st1[:, r, :]).then_inc(s_mv1, 1)

            def mod_widths():
                dve.wait_ge(s_modt, 1)
                m = bank["k"][:, 0:4 * B].rearrange("p (m b) -> p m b", b=B)
                dve.tensor_copy(mod_t[:, 0:DK, :], m[:, 0:DK, :])
                dve.tensor_scalar(mod_t[:, DK:2 * DK, :], m[:, DK:2 * DK, :], 1.0, None,
                                  ALU.add).then_inc(s_modt_ready, 1)

            def mod_rows():
                def gate(to, src):
                    step(dve.tensor_copy(raw_sb, src))
                    step(dve.tensor_scalar(sign_sb, raw_sb, 0.0, 2.0, ALU.is_ge, ALU.mult))
                    step(dve.scalar_tensor_tensor(mag_sb, raw_sb, -1.0, raw_sb, ALU.mult, ALU.max))
                    step(dve.tensor_scalar(mag_sb, mag_sb, 0.25, None, ALU.max))
                    step(dve.scalar_tensor_tensor(to, sign_sb, -1.0, mag_sb, ALU.add, ALU.mult))

                dve.wait_ge(s_modb, 1)
                gate(mod2_sb[:, 0:D], bank["kv0"][0:B, 0:D])
                step(dve.tensor_copy(mod2_sb[:, D:2 * D], bank["kv0"][0:B, D:2 * D]))
                step(dve.tensor_scalar(mod2_sb[:, 2 * D:3 * D], bank["kv1"][0:B, 0:D], 1.0, None, ALU.add))
                gate(mod2_sb[:, 3 * D:4 * D], bank["kv1"][0:B, D:2 * D])
                dve.memset(small[:, 51:52], 0.0).then_inc(s_modb_ready, 1)

            def b1_bound():
                dve.wait_ge(s_misc, 80)
                dve.tensor_reduce(b1_max, b1_sb[:], AX_X, ALU.max, apply_absolute_value=True).then_inc(s_bound, 1)

            def scale_of(largest, scale, unscale, s_step, base, s_to):
                dve.tensor_scalar(bits.bitcast(I32), largest.bitcast(I32), EXPONENT, None,
                                  ALU.bitwise_and).then_inc(s_step, 1)
                dve.wait_ge(s_step, base + 1)
                dve.tensor_scalar(scale.bitcast(I32), bits.bitcast(I32), -1.0, float((TOP + 254) * EXP_ONE),
                                  ALU.mult, ALU.add)
                dve.tensor_scalar(unscale.bitcast(I32), bits.bitcast(I32), float(-TOP * EXP_ONE), None,
                                  ALU.add).then_inc(s_to, 1)

            def token_scale():
                dve.wait_ge(s_modl, 16)
                step(dve.tensor_reduce(x_most[:, 0:1], scale_b, AX_XY, ALU.max, apply_absolute_value=True))
                step(dve.tensor_reduce(x_most[:, 1:2], shift_b, AX_XY, ALU.max, apply_absolute_value=True))
                step(dve.scalar_tensor_tensor(x_most[:, 2:3], x_most[:, 0:1], float(D) ** 0.5, x_most[:, 1:2],
                                              ALU.mult, ALU.add))
                step(dve.tensor_scalar(x_most[:, 3:4], x_most[:, 2:3], 2.0 ** -60, None, ALU.max))
                scale_of(x_most[:, 3:4], x_scale, x_unscale, s_xstep, 0, s_xscale)
                dve.wait_ge(s_xscale, 1)
                step(dve.tensor_scalar(hid_unit, x_scale, HID_SCALE, None, ALU.mult))
                step(dve.tensor_scalar(y_unit, x_unscale, 1.0 / HID_SCALE, None, ALU.mult))
                step(dve.memset(w_floor[:], 2.0 ** -60))
                dve.wait_ge(s_bmax, 1)
                step(dve.tensor_scalar(w_floor[:, 0:NM:2], b1_all, hid_unit, 2.0, ALU.mult, ALU.mult))
                step(dve.tensor_scalar(w_floor[:], w_floor[:], 2.0 ** -60, None, ALU.max))

            def consts16():
                dve.tensor_copy(c16[:, 0:P], con("before"))
                dve.tensor_copy(c16[:, P:2 * P], con("ones"))
                step(dve.tensor_copy(c16[:, 2 * P:3 * P + NT], cst[:, COLS["slot_no"][0]:COLS["tile_no"][1]]))

            def max_piece(k, u, j):
                if (m := matrix_at(k, MAX)) is None:
                    return
                i = 2 * u + j
                if i == 0:
                    dve.wait_ge(s_wraw, 16 * (m + 1))
                last = dve.tensor_reduce(piece_max[:, i:i + 1], raw_piece(m, i), AX_X, ALU.max,
                                         apply_absolute_value=True)
                if i == PIECES - 1:
                    last.then_inc(s_wmaxh, 1)
                    dve.wait_ge(s_wmaxh, 2 * m + 1)
                    dve.tensor_reduce(w_most, piece_max, AX_X, ALU.max).then_inc(s_wmaxh, 1)
                    dve.wait_ge(s_wmaxh, 2 * m + 2)
                    dve.tensor_tensor(w_most, w_most, w_floor[:, bass.ds(m, 1)], ALU.max).then_inc(s_wboth, 1)

            def lo_piece(k, u, j):
                if (m := matrix_at(k, LO)) is None:
                    return
                i = 2 * u + j
                dve.wait_ge(s_whi, PIECES * m + i + 1)
                last = dve.scalar_tensor_tensor(part_piece(m, 1, i), raw_piece(m, i), w_scale[:, bass.ds(m, 1)],
                                                part_piece(m, 0, i), ALU.mult, ALU.subtract)
                if i == PIECES - 1:
                    last.then_inc(s_wlo, 1)

            def slot(k, u):
                attend, score = att_item(k, u, ATTEND), att_item(k, u, SCORE)
                if attend:
                    n, g, r = attend
                    if n == 0:
                        dve.wait_ge(s_modl, 16)
                    dve.wait_ge(s_o, n + 1)
                    dve.tensor_scalar(den[:, r, 0:1], bank["o"][:, D:DZ], DEN_EPS, None, ALU.add).then_inc(s_den, 1)
                first_stats(k, u)
                if attend:
                    dve.wait_ge(s_den, n + 1)
                    dve.reciprocal(den[:, r, 1:2], den[:, r, 0:1]).then_inc(s_rden, 1)
                lo_piece(k, u, 0)
                if attend:
                    dve.wait_ge(s_rden, n + 1)
                    dve.scalar_tensor_tensor(attended[:, r, :], bank["o"][:, 0:D], den[:, r, 1:2], gate_a[:, r, :],
                                             ALU.mult, ALU.mult).then_inc(s_atn, 1)
                first_mean_var(k, u)
                if score:
                    n = score[0]
                    dve.wait_ge(s_sc, n + 1)
                    need(dve, s_o, n - 1)
                    dve.tensor_tensor(att[:, score[2], :], bank["va"][:, D:D + P], decay[:], ALU.mult).then_inc(s_att, 1)
                if attend:
                    n, g, r = attend
                    dve.wait_ge(s_atn, n + 1)
                    need(dve, s_sx[r], 16 * g)
                    need(dve, s_xn2, n - 1)
                    dve.tensor_tensor(x1_sb[:, r, :], attended[:, r, :], x_sb[:, r, g % 4, :],
                                      ALU.add).then_inc(s_x1, 1)
                    dve.wait_ge(s_kv, n + 1)
                    for h in range(DK):
                        last = dve.scalar_tensor_tensor(state[:, r, h, 0:DZ], state[:, r, h, 0:DZ],
                                                        power[:, P - 1:P], bank[f"kv{h}"][:, 0:DZ],
                                                        ALU.mult, ALU.add)
                    last.then_inc(s_state, 1)
                    dve.wait_ge(s_x1, n + 1)
                    dve.bn_stats(st2[:, r, :], x1_sb[:, r, :]).then_inc(s_st2, 1)
                if (k, u) == (0, 1):
                    token_scale()
                max_piece(k, u, 0)
                if attend:
                    need(dve, s_rs2, n - 1)
                    dve.wait_ge(s_st2, n + 1)
                    dve.bn_aggr(mv2[:, r, :], st2[:, r, :]).then_inc(s_mv2, 1)
                if it := att_item(k, u, LOGIT):
                    n, g, r = it
                    dve.wait_ge(s_lg, n + 1)
                    dve.tensor_tensor(logits[:, n, :], bank["h"][:, D:D + NE], br_sb[:], ALU.add).then_inc(s_lgr, 1)
                if it := att_item(k, u, PROJ):
                    n, g, r = it
                    dve.wait_ge(s_vp, n + 1)
                    if n == 0:
                        dve.wait_ge(s_init, INIT)
                    need(dve, s_kv, n - 1)
                    dve.tensor_tensor(v_ext[:, r, 0:D], bank["va"][:, 0:D], bv_sb[:], ALU.add).then_inc(s_v, 1)
                lo_piece(k, u, 1)
                if u == 0 and (m := matrix_at(k, HI)) is not None:
                    dve.wait_ge(s_wmax, m + 1)
                    scale_of(all_max, w_scale[:, m:m + 1], w_unscale[:, m:m + 1], s_wbits, m, s_wscale)
                if (k, u) == (-1, 0):
                    mod_widths()
                    b1_bound()
                    mod_rows()
                if (k, u) == (0, 0):
                    consts16()
                max_piece(k, u, 1)

            slots(dve, *ATT_S, slot)

            hops = [0]

            def hop(ins):
                hops[0] += 1
                ins.then_inc(s_route, 1)
                dve.wait_ge(s_route, hops[0])

            top = scratch[:, 0:NCH]
            hot = scratch[:, 64:64 + NCH * NE].rearrange("p (n e) -> p n e", e=NE)
            best = scratch[:, 320:320 + NCH]
            chosen_ne = chosen16.rearrange("p (e n) -> p n e", e=NE)
            upto = scratch[:, 640:640 + NE * NCH + 1]
            count = scratch[:, 900:900 + NE]
            full = scratch[:, 908:908 + NE]
            upto_tile = scratch[:, 916:916 + NE]
            first = scratch[:, 924:924 + NE]
            over = scratch[:, 1024:1280].rearrange("p (e n) -> p e n", e=NE)
            place = scratch[:, 1280:1536]
            pos = scratch[:, 1536:1568]
            pos_i = scratch[:, 1568:1600].bitcast(I32)
            pos_tile = scratch[:, 1600:1632].bitcast(I32)
            pos_slot_i = scratch[:, 1632:1664].bitcast(I32)
            pos_slot = scratch[:, 1664:1696]
            late = scratch[:, 1696:1696 + NT * NE].rearrange("p (t e) -> p t e", e=NE)
            tile_f = scratch[:, 2016:2016 + NT]
            token_f = scratch[:, 2056:2056 + NT]

            dve.wait_ge(s_lgr, NCH)
            for b in range(B):
                dve.wait_ge(s_sx[b], 16 * (NCH // B))
                dve.wait_ge(s_sh[b], 16 * (NCH // B))
            hop(dve.tensor_reduce(top, logits[:], AX_X, ALU.max))
            hop(dve.tensor_tensor(hot, logits[:], top.unsqueeze(2).to_broadcast([P, NCH, NE]), ALU.is_equal))
            hop(dve.tensor_tensor(hot, hot, con("weight8").unsqueeze(1).to_broadcast([P, NCH, NE]), ALU.mult))
            hop(dve.tensor_reduce(best, hot, AX_X, ALU.max))
            hop(dve.tensor_tensor(chosen_ne, hot, best.unsqueeze(2).to_broadcast([P, NCH, NE]), ALU.is_equal))
            dve.memset(upto[:, 0:1], 0.0).then_inc(s_chosen, 1)
            dve.wait_ge(s_rank, 1)
            one = con("ones")[:, 0:1]
            hop(dve.tensor_tensor_scan(upto[:, 1:1 + NE * NCH], one.to_broadcast([P, NE * NCH]), bank["va"][:, 0:NE * NCH], 0.0,
                                       ALU.mult, ALU.add))
            ends = upto[:, NCH:NE * NCH + 1:NCH]
            starts = upto[:, 0:NE * NCH:NCH]
            hop(dve.tensor_tensor(count, ends, starts, ALU.subtract))
            hop(dve.tensor_tensor(over, count.unsqueeze(2).to_broadcast([P, NE, NCH]),
                                  con("bounds").unsqueeze(1).to_broadcast([P, NE, NCH]), ALU.is_gt))
            hop(dve.tensor_reduce(full, over, AX_X, ALU.add))
            hop(dve.tensor_tensor_scan(upto_tile, one.to_broadcast([P, NE]), full, 0.0,
                                       ALU.mult, ALU.add))
            hop(dve.tensor_tensor(first, upto_tile, full, ALU.subtract))
            hop(dve.scalar_tensor_tensor(first, first, float(P), starts, ALU.mult, ALU.subtract))
            hop(dve.tensor_tensor(place, bank["qk"][:, 0:NE * NCH], upto[:, 0:NE * NCH], ALU.add))
            place_en = place.rearrange("p (e n) -> p e n", e=NE)
            hop(dve.tensor_tensor(place_en, place_en, first.unsqueeze(2).to_broadcast([P, NE, NCH]), ALU.add))
            hop(dve.tensor_tensor(place, place, chosen16, ALU.mult))
            hop(dve.tensor_reduce(pos, place.rearrange("p (e n) -> p n e", e=NE), AX_X, ALU.add))
            hop(dve.tensor_copy(pos_i, pos))
            hop(dve.tensor_scalar(pos_tile, pos_i, 7, None, ALU.arith_shift_right))
            hop(dve.tensor_scalar(pos_slot_i, pos_i, P - 1, None, ALU.bitwise_and))
            hop(dve.tensor_copy(pos_slot, pos_slot_i))
            hop(dve.tensor_tensor(hot_tile, pos_tile.unsqueeze(2).to_broadcast([P, NCH, NT]),
                                  con("tile_no").unsqueeze(1).to_broadcast([P, NCH, NT]), ALU.is_equal))
            dve.tensor_scalar(in_tile[:, :, 1, :], hot_tile, con("lane"), None, ALU.mult)
            hop(dve.tensor_tensor(in_tile[:, :, 0, :], hot_tile,
                                  con("chunk_less").unsqueeze(2).to_broadcast([P, NCH, NT]), ALU.mult))
            for n in range(NCH):
                last = dve.tensor_scalar(in_slot[:, n, :], slot_no16, pos_slot[:, n:n + 1], None, ALU.is_equal)
                if n % (NCH // 4) == NCH // 4 - 1:
                    last.then_inc(s_bits, 1)
            hop(dve.tensor_tensor(late[:, :, 0:NE - 1], con("tile_no").unsqueeze(2).to_broadcast([P, NT, NE - 1]),
                                  upto_tile[:, 0:NE - 1].unsqueeze(1).to_broadcast([P, NT, NE - 1]), ALU.is_ge))
            hop(dve.tensor_reduce(tile_f, late[:, :, 0:NE - 1], AX_X, ALU.add))
            hop(dve.tensor_scalar(tile_matrix[:], tile_f, 2.0, None, ALU.mult))
            dve.wait_ge(s_ids, 1)
            hop(dve.tensor_scalar(token_f, bank["x"][:, 0:NT], float(P), float(NTOK), ALU.mult, ALU.add))
            hop(dve.tensor_tensor(token_f, token_f, bank["x"][:, NT:2 * NT], ALU.add))
            hop(dve.tensor_copy(slot_token[:], token_f))
            hop(dve.tensor_scalar(slot_late[:], token_f, float(S), None, ALU.is_ge))
            dve.tensor_scalar(slot_early[:], token_f, float(S), None, ALU.is_lt).then_inc(s_routed, 1)

            dve.wait_ge(s_idx, 1)

            def hidden_lo(n, r, h):
                dve.wait_ge(s_hhi, 2 * n + h + 1)
                dve.tensor_tensor(hid_parts[:, r % 2, 1, 4 * h:4 * h + 4, :], hid[:, 4 * h:4 * h + 4, :],
                                  hid_parts[:, r % 2, 0, 4 * h:4 * h + 4, :], ALU.subtract).then_inc(s_hlo, 1)

            def last_tile(it):
                return isinstance(it[0], int) and it[0] == NT - 1

            def copy_w1(m, n, i):
                if i == 1:
                    need(dve, s_hp, 2 * n)
                of = w[:, bass.ds(m, 1)].rearrange("p a i (h f) -> p (a i h) f", h=DK)
                now = w1_now.rearrange("p i (h f) -> p (i h) f", h=DK)
                dve.tensor_copy(now[:, :, i * F // 2:(i + 1) * F // 2],
                                of[:, :, i * F // 2:(i + 1) * F // 2]).then_inc(s_w1, 1)

            def slot(k, u):
                if it := ffn_item(k, u, -1):
                    alone(dve, (s_hp, 2 * it[0] - 1))
                    m = dve.value_load(tile_matrix[0:1, bass.ds(it[0], 1)], min_val=0, max_val=NM - 2)
                    copy_w1(m, it[0], 0)
                    if cur := ffn_item(k, u, 0):
                        hidden_lo(cur[0], cur[2], 0)
                    copy_w1(m, it[0], 1)
                    n, g, r = it
                    dve.wait_ge(s_thi, n + 1)
                    dve.scalar_tensor_tensor(tok_parts[:, r % 2, 1],
                                             bank["h"][:, 0:D].rearrange("p (k t) -> p k t", k=DK), x_scale,
                                             tok_parts[:, r % 2, 0], ALU.mult, ALU.subtract).then_inc(s_tlo, 1)
                if it := ffn_item(k, u, 0):
                    if last_tile(it):
                        hidden_lo(it[0], it[2], 0)
                    hidden_lo(it[0], it[2], 1)
                if it := ffn_item(k, u, 1):
                    n, g, r = it
                    alone(dve, (s_out[r % 2], 16 * (2 * g + r // 2)), (s_y, n + 1))
                    m = dve.value_load(tile_matrix[0:1, bass.ds(n, 1)], min_val=0, max_val=NM - 2)
                    b2_of = b2_sb[:].rearrange("p e (a d) -> p (e a) d", a=2)[:, bass.ds(m, 2), :]
                    dve.scalar_tensor_tensor(done_rows[:, r % 2, :], bank["o"][:, 0:D], scale_now[:, r, 1:2],
                                             b2_of.rearrange("p a d -> p (a d)"), ALU.mult, ALU.add).then_inc(s_ys, 1)
                    dve.wait_ge(s_gate, n + 1)
                    dve.wait_ge(s_ys, 2 * n + 1)
                    dve.tensor_tensor(done_rows[:, r % 2, :], done_rows[:, r % 2, :], gate_now[:, r, :],
                                      ALU.mult).then_inc(s_ys, 1)

            slots(dve, *FFN, slot)

        @block.tensor
        def _(pe):
            pe.wait_ge(s_csilu, 1)
            pe.wait_ge(s_cmod, 16)
            for m in range(2 * DK):
                for k in range(DK):
                    last = pe.matmul(bank["k"][:, m * B:(m + 1) * B], wmod_sb[:, k, m * P:(m + 1) * P],
                                     c_silu[:, k, :], start=(k == 0), stop=(k == DK - 1))
            last.then_inc(s_modt, 1)

            for i in range(2):
                for k in range(DK):
                    last = pe.matmul(bank[f"kv{i}"][0:B, :], c_silu[:, k, :], wmod_sb[:, k, (i + 1) * 512:(i + 2) * 512],
                                     start=(k == 0), stop=(k == DK - 1))
            last.then_inc(s_modb, 1)

            def slot(k, u):
                if it := att_item(k, u, ATTEND):
                    n, g, r = it
                    if isinstance(n, int) and n == 0:
                        pe.wait_ge(s_init, INIT)
                        pe.wait_ge(s_modb_ready, 1)
                    pe.wait_ge(s_att, n + 1)
                    pe.wait_ge(s_v, n + 1)
                    need(pe, s_atn, n)
                    pe.matmul(bank["o"][:, 0:DZ], att[:, r, :], v_ext[:, r, 0:DZ], start=True, stop=False)
                    pe.wait_ge(s_qg, n + 1)
                    need(pe, s_state, n - 1)
                    for h in range(DK):
                        last = pe.matmul(bank["o"][:, 0:DZ], qg_t[:, r, h, :], state[:, r, h, 0:DZ],
                                         start=False, stop=(h == DK - 1))
                    last.then_inc(s_o, 1)
                    pe.wait_ge(s_kg, n + 1)
                    need(pe, s_state, n)
                    for h in range(DK):
                        last = pe.matmul(bank[f"kv{h}"][:, 0:DZ], kg[:, r, h * P:(h + 1) * P], v_ext[:, r, 0:DZ],
                                         start=True, stop=True)
                    last.then_inc(s_kv, 1)
                if it := att_item(k, u, LOGIT):
                    n, g, r = it
                    pe.wait_ge(s_h2t, n + 1)
                    for h in range(DK):
                        last = pe.matmul(bank["h"][:, D:D + NE], h2_t[:, r, h, :], wr_sb[:, h, :],
                                         start=(h == 0), stop=(h == DK - 1))
                    last.then_inc(s_lg, 1)
                if it := att_item(k, u, SCORE):
                    n, g, r = it
                    pe.wait_ge(s_k, n + 1)
                    need(pe, s_kg, n)
                    for h in range(DK):
                        last = pe.transpose(bank["k"][:, h * P:(h + 1) * P], k_t[:, r, h, :], ident)
                    last.then_inc(s_kx, 1)
                    pe.wait_ge(s_v, n + 1)
                    for h in range(DK):
                        last = pe.matmul(bank["va"][:, D:D + P], k_t[:, r, h, :], q_t[:, r, h, :],
                                         start=(h == 0), stop=(h == DK - 1))
                    last.then_inc(s_sc, 1)
                if it := att_item(k, u, PROJ):
                    n, g, r = it
                    if isinstance(n, int) and n == 0:
                        pe.wait_ge(s_wqkv, 32)
                    pe.wait_ge(s_ht, n + 1)
                    need(pe, s_k, n)
                    for m in range(2):
                        for c in range(DK):
                            for h in range(DK):
                                last = pe.matmul(bank["qk"][:, (m * DK + c) * P:(m * DK + c + 1) * P],
                                                 wqkv_sb[:, m, h, c * P:(c + 1) * P], h_t[:, r, h, :],
                                                 start=(h == 0), stop=(h == DK - 1))
                    last.then_inc(s_qkp, 1)
                    need(pe, s_att, n)
                    for h in range(DK):
                        last = pe.matmul(bank["va"][:, 0:D], h_t[:, r, h, :], wqkv_sb[:, 2, h, :],
                                         start=(h == 0), stop=(h == DK - 1))
                    last.then_inc(s_vp, 1)
                if it := att_item(k, u, XPOSE2):
                    n, g, r = it
                    pe.wait_ge(s_h2, n + 1)
                    need(pe, s_h2t, n)
                    need(pe, s_lgr, n)
                    for h in range(DK):
                        last = pe.transpose(bank["h"][:, h * P:(h + 1) * P], h2[:, r, h * P:(h + 1) * P], ident)
                    last.then_inc(s_h2x, 1)
                if it := att_item(k, u, XPOSE):
                    n, g, r = it
                    if isinstance(n, int) and n == 0:
                        pe.wait_ge(s_const, 16)
                    pe.wait_ge(s_xn1, n + 1)
                    need(pe, s_ht, n)
                    for h in range(DK):
                        last = pe.transpose(bank["x"][:, h * P:(h + 1) * P], xn1[:, r, h * P:(h + 1) * P], ident)
                    last.then_inc(s_xt, 1)
            slots(pe, *ATT, slot)

            pe.wait_ge(s_chosen, 1)
            pe.matmul(bank["qk"][:, 0:NE * NCH], before16, chosen16, start=True, stop=True)
            pe.matmul(bank["va"][:, 0:NE * NCH], ones16, chosen16, start=True, stop=True).then_inc(s_rank, 1)
            for n in range(NCH):
                if n % (NCH // 4) == 0:
                    pe.wait_ge(s_bits, n // (NCH // 4) + 1)
                last = pe.matmul(bank["x"][:, 0:2 * NT], in_slot[:, n, :],
                                 in_tile[:, n].rearrange("p i t -> p (i t)"), start=(n == 0), stop=(n == NCH - 1))
            last.then_inc(s_ids, 1)

            pe.wait_ge(s_routed, 1)
            pe.wait_ge(s_wlo, NM)

            parts = ((0, 0), (0, 1), (1, 0))

            def slot(k, u):
                if it := ffn_item(k, u, 0):
                    n, g, r = it
                    pe.wait_ge(s_tlo, n + 1)
                    for i, name in enumerate(("qk", "va")):
                        pe.wait_ge(s_w1, 2 * n + i + 1)
                        need(pe, s_ha, 2 * n + i - 1)
                        for f in range(4 * i, 4 * i + 4):
                            for q, (a, b) in enumerate(parts):
                                for h in range(DK):
                                    at_w = h * F + f * P
                                    last = pe.matmul(bank[name][:, (f % 4) * P:(f % 4 + 1) * P],
                                                     w1_now[:, a, at_w:at_w + P], tok_parts[:, r % 2, b, h, :],
                                                     start=(q == 0 and h == 0), stop=(q == 2 and h == DK - 1))
                        last.then_inc(s_hp, 1)
                if it := ffn_item(k, u, -1):
                    n, g, r = it
                    pe.wait_ge(s_in[r], 16 * (g + 1))
                    need(pe, s_tlo, n)
                    for h in range(DK):
                        last = pe.transpose(bank["h"][:, h * P:(h + 1) * P],
                                            tok[:, r, D + h * P:D + (h + 1) * P], ident)
                    last.then_inc(s_tx, 1)
                if it := ffn_item(k, u, 1):
                    n, g, r = it
                    m = pe.value_load(tile_matrix[0:1, bass.ds(n, 1)], min_val=0, max_val=NM - 2)
                    pe.wait_ge(s_hlo, 2 * n + 2)
                    need(pe, s_ys, 2 * n - 1)
                    for f in range(FK):
                        for q, (a, b) in enumerate(parts):
                            last = pe.matmul(bank["o"][:, 0:D], hid_parts[:, r % 2, b, f, :],
                                             w[:, bass.ds(m + 1, 1), a, f * D:(f + 1) * D].rearrange("p a d -> p (a d)"),
                                             start=(f == 0 and q == 0), stop=(f == FK - 1 and q == 2))
                    last.then_inc(s_y, 1)

            slots(pe, *FFN, slot)


def kernel(L0_attn_x_seq, L0_attn_Wq, L0_attn_bq, L0_attn_Wk, L0_attn_bk, L0_attn_Wv, L0_attn_bv, L0_attn_gamma,
           L0_ffn_Wr, L0_ffn_br, L0_ffn_W1, L0_ffn_b1, L0_ffn_W2, L0_ffn_b2, L0_c, L0_wmod):
    import concourse.bacc as bacc
    from concourse.bass_utils import run_bass_kernel_spmd

    def by_width(a):
        a = np.asarray(a)
        return np.moveaxis(a.reshape(*a.shape[:-1], -1, P), -1, 0)

    def rows_of(a, shape):
        return np.broadcast_to(np.asarray(a).reshape(1, -1), (P, int(np.prod(shape)))).reshape(P, *shape)

    qkv = np.stack([np.asarray(w) for w in (L0_attn_Wq, L0_attn_Wk, L0_attn_Wv)])
    consts = constants()
    laid = {
        "x": np.asarray(L0_attn_x_seq).reshape(NTOK, D),
        "wqkv": by_width(qkv).transpose(0, 1, 3, 2),
        "bqk": by_width(np.stack([np.asarray(L0_attn_bq), np.asarray(L0_attn_bk)])),
        "bvb": rows_of(L0_attn_bv, (D,)),
        "gamma": rows_of(L0_attn_gamma, (1,)),
        "wr": by_width(L0_ffn_Wr).transpose(0, 2, 1),
        "brb": rows_of(L0_ffn_br, (NE,)),
        "w_raw": np.stack([
            by_width(L0_ffn_W1).transpose(1, 0, 3, 2).reshape(NE, P, MW),
            by_width(L0_ffn_W2).transpose(1, 0, 3, 2).reshape(NE, P, MW),
        ], 1).reshape(NM, P, MW),
        "b1": by_width(L0_ffn_b1),
        "b2b": rows_of(L0_ffn_b2, (NE, D)),
        "c_t": by_width(L0_c).transpose(0, 2, 1),
        "wmod": np.asarray(L0_wmod).reshape(DK, P, 6 * D).transpose(1, 0, 2),
        "consts": consts,
    }
    nc = bacc.Bacc("TRN2", target_bir_lowering=False, num_devices=1)
    arrays, args = {}, []
    for name, a in laid.items():
        a = np.ascontiguousarray(a)
        arrays[f"in_{name}"] = a
        args.append(nc.dram_tensor(f"in_{name}", a.shape, mybir.dt.from_np(a.dtype), kind="ExternalInput").ap())
    args.append(nc.dram_tensor("out_rows", (NTOK, D), F32, kind="ExternalOutput").ap())
    build(nc, *args)
    r = run_bass_kernel_spmd(nc, [arrays], core_ids=[0])
    return r.results[0]["out_rows"].reshape(B, S, D)
```

```python
from contextlib import ExitStack

import numpy as np

import concourse.bass as bass
from concourse import mybir

F32 = mybir.dt.float32
F16 = mybir.dt.float16
I32 = mybir.dt.int32
ALU = mybir.AluOpType
ACT = mybir.ActivationFunctionType
AX_X = mybir.AxisListType.X

P = 128
B, S, D = 2, 2048, 256
DK = D // P
NE, F = 8, 1024
FK = F // P
NTOK = B * S
NCH = NTOK // P
NT = NCH + NE - 1
DZ = D + 1
LN_EPS, DEN_EPS = 1e-5, 1e-6
INIT = B * (DK + 1) + 3

LOAD, STATS, NORM, XPOSE, PROJ, SCORE, ATTEND, NORM2, XPOSE2, LOGIT = -6, -3, -2, -1, 0, 1, 2, 3, 4, 5
COLS = {}
_at = 0
for _name, _n in (("ident", P), ("before", P), ("ones", P), ("slot_no", P), ("tile_no", NT), ("weight8", NE),
                  ("chunk_less", NCH), ("lane", 1)):
    COLS[_name] = (_at, _at + _n)
    _at += _n
NCONST = _at
NM = 2 * NE
MW = DK * F
ACT_CHUNKS = 8
TOP = 14
EXPONENT = 0x7F800000
EXP_ONE = 1 << 23
HID_SCALE = 2.0 ** -23


def constants():
    p = np.arange(P)
    c = np.zeros((P, NCONST), np.float32)

    def put(name, value):
        a, b = COLS[name]
        c[:, a:b] = value

    put("ident", np.eye(P))
    put("before", p[:, None] < p[None, :])
    put("ones", 1.0)
    put("slot_no", p[None, :])
    put("tile_no", np.arange(NT)[None, :])
    put("weight8", NE - np.arange(NE)[None, :])
    n = np.arange(NCH)
    put("chunk_less", ((n % B) * (S // P) + n // B - NTOK // P)[None, :])
    put("lane", p[:, None])
    return c


def need(eng, sem, count):
    if isinstance(count, int) and count <= 0:
        return
    eng.wait_ge(sem, count)


def slots(eng, unroll, first, loop, last, slot):
    for k in range(first, loop[0]):
        for u in range(unroll):
            slot(k, u)
    if loop[1] > loop[0]:
        with eng.Fori(loop[0], loop[1], 1) as k:
            for u in range(unroll):
                slot(k, u)
    for k in range(loop[1], last + 1):
        for u in range(unroll):
            slot(k, u)


def item(k, u, lag, unroll, count):
    q, r = divmod(u - lag, unroll)
    g = k + q
    n = g * unroll + r
    if isinstance(n, int) and not 0 <= n < count:
        return None
    return n, g, r


ATT = (B, -3, (4, 13), 18)
ATT_S = (B, -3, (4, 4), 18)
FFN = (4, -1, (2, 9), 9)
MAX, HI, LO = 0, 1, 2
PIECES = 4
STAGES = 4


def build(nc, x, wqkv, bqk, bvb, gamma, wr, brb, w_raw, b1, b2b, c_t, wmod, consts, out):
    rows = nc.dram_tensor("token_rows", [NTOK, 2 * D], F32, kind="Internal").ap()
    mods = nc.dram_tensor("mod_rows", [1, B * 4 * D], F32, kind="Internal").ap()
    with ExitStack() as ctx:
        def sb(name, shape, dt=F32):
            return ctx.enter_context(nc.sbuf_tensor(name, shape, dt))

        def sem(name):
            return ctx.enter_context(nc.semaphore(name))

        bank = {n: ctx.enter_context(nc.psum_tensor(f"ps_{n}", [P, 512], F32))
                for n in ("o", "kv0", "kv1", "qk", "va", "x", "h", "k")}

        w = sb("w", [P, NM + 1, 2, MW], F16)
        w_scale = sb("w_scale", [P, NM])
        w_unscale = sb("w_unscale", [P, NM])
        w_floor = sb("w_floor", [P, NM])
        cst = sb("cst", [P, NCONST])
        wqkv_sb = sb("wqkv_sb", [P, 3, DK, D])
        bqk_sb = sb("bqk_sb", [P, 2, DK])
        bv_sb = sb("bv_sb", [P, D])
        wr_sb = sb("wr_sb", [P, DK, NE])
        br_sb = sb("br_sb", [P, NE])
        b1_sb = sb("b1_sb", [P, NE, FK])
        b2_sb = sb("b2_sb", [P, NE, D])
        mod_t = sb("mod_t", [P, 2 * DK, B])
        mod_rows_sb = sb("mod_rows_sb", [P, B, 4, D])
        gate_a, shift_b, scale_b, gate_b = (mod_rows_sb[:, :, i, :] for i in range(4))
        logits = sb("logits", [P, NCH, NE])
        power = sb("power", [P, P])
        decay = sb("decay", [P, P])
        slot_token = sb("slot_token", [P, NT], I32)
        slot_late = sb("slot_late", [P, NT])
        slot_early = sb("slot_early", [P, NT])
        tile_matrix = sb("tile_matrix", [P, NT], I32)

        arena = sb("arena", [P, 9216])
        at = [0]

        def cut(*shape):
            n = int(np.prod(shape))
            v = arena[:, at[0]:at[0] + n]
            at[0] += n
            assert at[0] <= 9216, at
            if len(shape) == 2:
                v = v.rearrange("p (a b) -> p a b", a=shape[0])
            if len(shape) == 3:
                v = v.rearrange("p (a b c) -> p a b c", a=shape[0], b=shape[1])
            return v

        x_sb = cut(B, 4, D)
        xn1 = cut(B, D)
        h_t = cut(B, DK, P)
        q_t = cut(B, DK, P)
        k_t = cut(B, DK, P)
        qg_t = cut(B, DK, P)
        kg = cut(B, D)
        v_ext = cut(B, DZ + 1)
        att = cut(B, P)
        x1_sb = cut(B, D)
        xn2 = cut(B, D)
        h2 = cut(B, D)
        h2_t = cut(B, DK, P)
        state = cut(B, DK, DZ + 1)
        small = sb("small", [P, 64])
        st1, st2 = sb("st1", [P, B, 6]), sb("st2", [P, B, 6])
        mv1, mv2 = sb("mv1", [P, B, 2]), sb("mv2", [P, B, 2])
        rs1, rs2 = sb("rs1", [P, B, 4]), sb("rs2", [P, B, 4])
        den = sb("den", [P, B, 2])
        attended = sb("attended", [P, B, D])
        att_end = at[0]

        at[0] = 0
        tok = cut(4, 2 * D)
        hid = cut(FK, P)
        done_rows = cut(2, D)
        gate_now = cut(4, D)
        gate_part = cut(2, 2, D)
        tok_s = cut(2, DK * P)
        hid_s = cut(2, FK * P)
        b1_now = cut(4, FK)
        assert at[0] <= 9216
        idx_in = sb("idx_in", [P, 4], I32)
        idx_out = sb("idx_out", [P, 2], I32)

        tok_parts = tok_s.bitcast(F16).rearrange("p r (i k t) -> p r i k t", i=2, k=DK)
        hid_parts = hid_s.bitcast(F16).rearrange("p r (i f t) -> p r i f t", i=2, f=FK)
        w1_now = w[:, NM]
        scale_now = sb("scale_now", [P, 4, 2])

        spare = w[:, 10:13].rearrange("p m i c -> p (m i c)").bitcast(F32)
        wmod_sb = spare[:, 0:DK * 6 * D].rearrange("p (k m) -> p k m", k=DK)
        _o = DK * 6 * D
        c_sb = spare[:, _o:_o + 4].rearrange("p (k b) -> p k b", k=DK)
        c_exp = spare[:, _o + 4:_o + 8].rearrange("p (k b) -> p k b", k=DK)
        c_silu = spare[:, _o + 8:_o + 12].rearrange("p (k b) -> p k b", k=DK)
        sign_sb = spare[0:B, _o + 16:_o + 16 + D]
        mag_sb = spare[0:B, _o + 16 + D:_o + 16 + 2 * D]
        raw_sb = spare[0:B, _o + 16 + 2 * D:_o + 16 + 3 * D]
        mod2_sb = spare[0:B, _o + 16 + 3 * D:_o + 16 + 7 * D]
        raw_w = w[:].rearrange("p m i c -> p m (i c)").bitcast(F32)
        gamma_sb, fixed = small[:, 0:1], small[:, 8:11]
        x_scale, x_unscale = small[:, 12:13], small[:, 13:14]
        b1_max, b1_all = small[:, 16:16 + NE], small[:, 24:24 + NE]
        piece_max, w_most, all_max = small[:, 52:52 + PIECES], small[:, 34:35], small[:, 35:36]
        bits, x_most, x_all = small[:, 36:37], small[:, 40:44], small[:, 56:58]
        lane_max = small[:, 58:59]
        hid_unit, y_unit = small[:, 44:45], small[:, 45:46]
        c16 = sb("c16", [P, 3 * P + NT], F16)
        before16, ones16 = c16[:, 0:P], c16[:, P:2 * P]
        slot_no16, tile_no16 = c16[:, 2 * P:3 * P], c16[:, 3 * P:3 * P + NT]

        def con(name):
            a, b = COLS[name]
            return cst[:, a:b]

        ident = con("ident")

        s_const, s_x = sem("constants_landed"), [sem(f"x_landed_{b}") for b in range(B)]
        s_cmod = [sem(f"wmod_part_landed_{i}") for i in range(3)]
        s_gamma, s_wqkv, s_misc, s_b2 = (sem("gamma_landed"), sem("wqkv_landed"), sem("biases_landed"),
                                         sem("b2_landed"))
        s_wfloor = sem("w_max_floored")
        s_start, s_hot, s_minus, s_numbers, s_distance, s_act_bits, s_tokens = map(sem, (
            "ranks_start", "tiles_hot", "minus_slot_ready", "token_numbers_ready", "slot_distance_ready",
            "last_slots_hot", "slot_tokens_ready"))
        s_xbound, s_xmost, s_xall = sem("x_bound_cleared"), sem("x_bound_lane"), sem("x_bound_all")
        s_wraw, s_c = sem("w_raw_landed"), sem("c_landed")
        (s_wmaxh, s_wboth, s_wmax, s_wbits, s_wscale, s_whi, s_wlo) = map(sem, (
            "w_max_halves", "w_max_lane", "w_max_all", "w_scale_step", "w_scale_ready", "w_hi_ready", "w_lo_ready"))
        s_ready = sem("tile_constants_all_ready")
        s_w1 = sem("w1_half_copied")
        s_gpart, s_gate = sem("gate_part_ready"), sem("gate_ready")
        s_modd, s_modl, s_bound, s_bmax, s_xstep, s_xscale, s_hhi, s_hlo, s_thi, s_tlo = map(sem, (
            "mod_rows_in_dram", "mod_rows_landed", "b1_max_lane", "b1_max_all", "x_scale_step", "x_scale_ready",
            "hid_hi_ready", "hid_lo_ready", "tok_hi_ready", "tok_lo_ready"))
        s_cexp, s_csilu, s_modt, s_modt_ready = (sem("c_exp_ready"), sem("c_silu_ready"), sem("mod_t_done"),
                                                 sem("mod_t_ready"))
        s_modb, s_modb_ready, s_setup = sem("mod_rows_done"), sem("mod_rows_ready"), sem("setup_step")
        s_marks = sem("marks")
        s_decay, s_init = sem("decay_ready"), sem("state_cleared")
        (s_st1, s_mv1, s_rs1s, s_rs1, s_xn1, s_xt, s_ht) = map(sem, (
            "stats1", "mean_var1", "rstd1_step", "rstd1", "xn1_ready", "x_transposed", "h_t_ready"))
        (s_qkp, s_vp, s_q, s_k, s_qg, s_v) = map(sem, (
            "qk_projected", "v_projected", "q_ready", "k_ready", "qg_ready", "v_ready"))
        (s_kx, s_kg, s_sc, s_att) = map(sem, ("k_transposed", "kg_ready", "scores_done", "att_ready"))
        (s_o, s_kv, s_state, s_den, s_rden, s_atn, s_x1) = map(sem, (
            "attended_done", "kv_done", "state_ready", "den_ready", "rden_ready", "attended_ready", "x1_ready"))
        (s_st2, s_mv2, s_rs2s, s_rs2, s_xn2, s_h2s, s_h2) = map(sem, (
            "stats2", "mean_var2", "rstd2_step", "rstd2", "xn2_ready", "h2_step", "h2_ready"))
        (s_h2x, s_h2t, s_lg, s_lgr) = map(sem, ("h2_transposed", "h2_t_ready", "logits_done", "logits_ready"))
        s_sx = [sem(f"x1_stored_{b}") for b in range(B)]
        s_sh = [sem(f"h2_stored_{b}") for b in range(B)]
        s_route, s_chosen, s_rank, s_bits, s_ids, s_routed = map(sem, (
            "route_step", "chosen_ready", "ranks_done", "slots_hot", "ids_done", "routed"))
        s_in = [sem(f"tokens_gathered_{r}") for r in range(4)]
        s_out = [sem(f"rows_scattered_{r}") for r in range(2)]
        (s_idx, s_prep, s_preps, s_tx, s_hp, s_ha, s_y, s_ys, s_done) = map(sem, (
            "index_copied", "tile_constants_step", "rows_index_copied", "tokens_transposed",
            "hidden_done", "hidden_ready", "y_done", "y_step", "rows_done"))

        scratch = arena[:, 4 * 2 * D:9216]
        chosen16 = scratch[:, 384:512].bitcast(F16)
        top, best = scratch[:, 0:NCH], scratch[:, 320:320 + NCH]
        hot = scratch[:, 64:64 + NCH * NE].rearrange("p (n e) -> p n e", e=NE)
        chosen_ne = chosen16.rearrange("p (e n) -> p n e", e=NE)
        minus_slot = scratch[:, 3392 + NCH * NT // 2:3392 + NCH * NT // 2 + NCH]
        distance = scratch[:, 6144:7168].rearrange("p (n s) -> p n s", s=P)
        in_tile = scratch[:, 2112:2112 + NCH * NT].bitcast(F16).rearrange("p (n i t) -> p n i t", i=2, t=NT)
        hot_tile = scratch[:, 3392:3392 + NCH * NT // 2].bitcast(F16).rearrange("p (n t) -> p n t", t=NT)
        in_slot = scratch[:, 4096:4096 + NCH * P // 2].bitcast(F16).rearrange("p (n s) -> p n s", s=P)

        block = ctx.enter_context(nc.Block())

        def att_item(k, u, lag):
            return item(k, u, lag, B, NCH)

        def ffn_item(k, u, lag):
            return item(k, u, lag, FFN[0], NT)

        def alone(eng, *waits):
            for w, c in waits:
                need(eng, w, c)
                eng.sem_inc(s_marks, 1)

        def matrix_at(k, lag):
            m = k - lag
            return m if not isinstance(m, int) or 0 <= m < NM else None

        def landing(m):
            return (m + STAGES - 1 - (NM - 1) % STAGES) % STAGES + NM + 1 - STAGES

        def piece(v, i):
            return v[:, i * (MW // PIECES):(i + 1) * (MW // PIECES)]

        def raw_piece(m, i):
            return piece(raw_w[:, bass.ds(landing(m), 1), :].rearrange("p a c -> p (a c)"), i)

        def part_piece(m, part, i):
            return piece(w[:, bass.ds(m, 1), part, :].rearrange("p a c -> p (a c)"), i)

        def load_matrix(eng, m):
            alone(eng, (s_wraw, 16 * m), (s_wlo, m - STAGES + 1))
            eng.dma_start(raw_w[:, bass.ds(landing(m), 1), :].rearrange("p a c -> p (a c)"),
                          w_raw[bass.ds(m, 1)].rearrange("a p c -> p (a c)")).then_inc(s_wraw, 16)

        def token_row(g, r):
            return r * S + g * P

        @block.sync
        def _(sp):
            sp.dma_start(c_sb, c_t).then_inc(s_c, 16)

            def slot(k, u):
                if it := att_item(k, u, LOAD):
                    n, g, r = it
                    alone(sp, (s_x[r], g * 16), (s_x1, n - 7))
                    sp.dma_start(x_sb[:, r, bass.ds(g % 4, 1), :].rearrange("p a d -> p (a d)"),
                                 x[bass.ds(token_row(g, r), P), :]).then_inc(s_x[r], 16)
                    if isinstance(n, int) and n == 0:
                        sp.dma_start(cst[:], consts).then_inc(s_const, 16)
                    if isinstance(n, int) and n == 1:
                        sp.dma_start(wqkv_sb[:], wqkv).then_inc(s_wqkv, 16)
                        sp.dma_start(bqk_sb[:], bqk).then_inc(s_wqkv, 16)
                        sp.dma_start(bv_sb[:], bvb).then_inc(s_misc, 16)
                        sp.dma_start(wr_sb[:], wr).then_inc(s_misc, 16)
                        sp.dma_start(br_sb[:], brb).then_inc(s_misc, 16)
                        sp.dma_start(b1_sb[:], b1).then_inc(s_misc, 16)
                if u == 1 and isinstance(k, int) and -2 <= k < STAGES - 2:
                    load_matrix(sp, k + 2)
                if u == 0 and (not isinstance(k, int) or STAGES - 1 <= k < NM - 1):
                    load_matrix(sp, k + 1)
                if it := att_item(k, u, ATTEND):
                    n, g, r = it
                    alone(sp, (s_sx[r], g * 16), (s_x1, n + 1))
                    sp.dma_start(rows[bass.ds(token_row(g, r), P), 0:D], x1_sb[:, r, :]).then_inc(s_sx[r], 16)
                if isinstance(k, int) and k in (-1, 0) and u == 1:
                    i, (a, b) = k + 2, ((0, D), (D, 4 * D))[k + 1]
                    sp.wait_ge(s_modb_ready, i)
                    if i == 2:
                        sp.wait_ge(s_modl, 16)
                    sp.dma_start(mods.rearrange("a (b m) -> (a b) m", b=B)[:, a:b], mod2_sb[:, a:b]).then_inc(s_modd, 16)
                    sp.wait_ge(s_modd, 16 * i)
                    sp.dma_start(mod_rows_sb[:].rearrange("p b m d -> p b (m d)")[:, :, a:b],
                                 mods.rearrange("a (b m) -> a b m", b=B)[:, :, a:b].to_broadcast([P, B, b - a])
                                 ).then_inc(s_modl, 16)
                if isinstance(k, int) and (k, u) == (1, 0):
                    sp.dma_start(b2_sb[:], b2b).then_inc(s_b2, 16)
                if it := att_item(k, u, NORM2):
                    n, g, r = it
                    alone(sp, (s_sh[r], g * 16), (s_h2, n + 1))
                    sp.dma_start(rows[bass.ds(token_row(g, r), P), D:2 * D], h2[:, r, :]).then_inc(s_sh[r], 16)

            slots(sp, *ATT, slot)

        @block.gpsimd
        def _(pool):
            for b in range(B):
                for k in range(DK):
                    pool.memset(state[:, b, k, :], 0.0).then_inc(s_init, 1)
                pool.memset(v_ext[:, b, D:DZ], 1.0).then_inc(s_init, 1)

            def inverse_deviation(n, r, s_mv, mv, rs, s_step, s_free, s_ready):
                pool.wait_ge(s_mv, n + 1)
                need(pool, s_free, n - 1)
                pool.tensor_tensor(rs[:, r, 0:1], mv[:, r, 1:2], fixed[:, 1:2], ALU.add).then_inc(s_step, 1)
                pool.wait_ge(s_step, 3 * n + 1)
                pool.tensor_tensor(rs[:, r, 1:2], rs[:, r, 0:1], fixed[:, 0:1], ALU.pow).then_inc(s_step, 1)
                pool.wait_ge(s_step, 3 * n + 2)
                pool.tensor_tensor(rs[:, r, 3:4], mv[:, r, 0:1], rs[:, r, 1:2], ALU.mult).then_inc(s_step, 1)
                pool.wait_ge(s_step, 3 * n + 3)
                pool.tensor_tensor(rs[:, r, 2:3], rs[:, r, 3:4], fixed[:, 2:3], ALU.mult).then_inc(s_ready, 1)

            for i, value in enumerate((-0.5, LN_EPS, -1.0)):
                pool.memset(fixed[:, i:i + 1], value).then_inc(s_init, 1)
            pool.wait_ge(s_init, INIT)

            def slot(k, u):
                if it := att_item(k, u, NORM):
                    n, g, r = it
                    inverse_deviation(n, r, s_mv1, mv1, rs1, s_rs1s, s_xn1, s_rs1)
                if it := att_item(k, u, NORM2):
                    n, g, r = it
                    inverse_deviation(n, r, s_mv2, mv2, rs2, s_rs2s, s_xn2, s_rs2)
                    if isinstance(n, int) and n == 0:
                        pool.wait_ge(s_modl, 32)
                    pool.wait_ge(s_xn2, n + 1)
                    need(pool, s_h2x, n - 1)
                    need(pool, s_sh[r], 16 * g)
                    pool.tensor_tensor(xn2[:, r, :], xn2[:, r, :], scale_b[:, r, :], ALU.mult).then_inc(s_h2s, 1)
                    pool.wait_ge(s_h2s, n + 1)
                    pool.tensor_tensor(h2[:, r, :], xn2[:, r, :], shift_b[:, r, :], ALU.add).then_inc(s_h2, 1)
                if isinstance(k, int) and (k, u) == (1, 0):
                    pool.wait_ge(s_bound, 1)
                    pool.partition_all_reduce(b1_all, b1_max, P, bass.bass_isa.ReduceOp.max).then_inc(s_bmax, 1)
                    pool.wait_ge(s_xmost, 1)
                    pool.partition_all_reduce(x_all, x_most[:, 0:2], P, bass.bass_isa.ReduceOp.max).then_inc(s_xall, 1)
                if u == 0 and (m := matrix_at(k, MAX + 1)) is not None:
                    alone(pool, (s_wboth, m + 1))
                    pool.partition_all_reduce(all_max, lane_max, P, bass.bass_isa.ReduceOp.max).then_inc(s_wmax, 1)
                if it := att_item(k, u, PROJ):
                    n, g, r = it
                    if isinstance(n, int) and n == 0:
                        pool.wait_ge(s_decay, 1)
                    pool.wait_ge(s_q, n + 1)
                    need(pool, s_o, n - 1)
                    pool.tensor_tensor(qg_t[:, r], q_t[:, r],
                                       power[:].unsqueeze(1).to_broadcast([P, DK, P]),
                                       ALU.mult).then_inc(s_qg, 1)

            slots(pool, *ATT, slot)

            for b in range(B):
                pool.wait_ge(s_sx[b], 16 * (NCH // B))
                pool.wait_ge(s_sh[b], 16 * (NCH // B))
            pool.wait_ge(s_x1, NCH)
            pool.memset(tok, 0.0).then_inc(s_idx, 1)
            pool.wait_ge(s_hot, 1)
            pool.tensor_tensor(in_tile[:, :, 0, :], hot_tile, con("chunk_less").unsqueeze(2).to_broadcast([P, NCH, NT]),
                               ALU.mult).then_inc(s_numbers, 1)
            pool.wait_ge(s_idx, 1)
            pool.wait_ge(s_tokens, 1)

            def slot(k, u):
                if it := ffn_item(k, u, -1):
                    n, g, r = it
                    pool.wait_ge(s_gpart, n + 1)
                    need(pool, s_done, n - 3)
                    pool.tensor_tensor(gate_now[:, r, :], gate_part[:, r % 2, 0, :], gate_part[:, r % 2, 1, :],
                                       ALU.add).then_inc(s_gate, 1)
                if it := ffn_item(k, u, 1):
                    n, g, r = it
                    landed = 16 * (2 * g + r // 2)
                    need(pool, s_out[r % 2], landed)
                    pool.tensor_copy(idx_out[:, r % 2:r % 2 + 1], slot_token[:, bass.ds(n, 1)]).then_inc(s_preps, 1)
                    pool.wait_ge(s_ys, 2 * n + 2)
                    pool.tensor_tensor(done_rows[:, r % 2, :], done_rows[:, r % 2, :], tok[:, r, 0:D],
                                       ALU.add).then_inc(s_done, 1)
                    alone(pool, (s_preps, n + 1), (s_done, n + 1))
                    pool.indirect_dma_start(out, bass.IndirectOffsetOnAxis(idx_out[:, r % 2:r % 2 + 1], 0),
                                            done_rows[:, r % 2, :], None, bounds_check=NTOK - 1,
                                            oob_is_err=False).then_inc(s_out[r % 2], 16)
                if it := ffn_item(k, u, -3):
                    n, g, r = it
                    need(pool, s_done, n - 3)
                    pool.tensor_copy(idx_in[:, r:r + 1], slot_token[:, bass.ds(n, 1)]).then_inc(s_idx, 1)
                    alone(pool, (s_idx, n + 2), (s_in[r], 16 * g))
                    pool.indirect_dma_start(tok[:, r, :], None, rows,
                                            bass.IndirectOffsetOnAxis(idx_in[:, r:r + 1], 0),
                                            bounds_check=NTOK - 1, oob_is_err=False).then_inc(s_in[r], 16)
                    if isinstance(n, int) and n == 0:
                        pool.wait_ge(s_routed, 1)
                    m = pool.value_load(tile_matrix[0:1, bass.ds(n, 1)], min_val=0, max_val=NM - 2)
                    b1_of = b1_sb[:].rearrange("p e (a f) -> p (e a) f", a=2)[:, bass.ds(m, 2), :]
                    pool.tensor_tensor(b1_now[:, r, :], b1_of.rearrange("p a f -> p (a f)"),
                                       w_scale[:, bass.ds(m, 1)].to_broadcast([P, FK]), ALU.mult).then_inc(s_prep, 1)
                    pool.tensor_tensor(scale_now[:, r, 0:1], w_unscale[:, bass.ds(m, 1)],
                                       w_unscale[:, bass.ds(m + 1, 1)], ALU.mult).then_inc(s_prep, 1)
                    pool.wait_ge(s_prep, 2 * n + 2)
                    pool.tensor_tensor(b1_now[:, r, :], b1_now[:, r, :], hid_unit.to_broadcast([P, FK]), ALU.mult)
                    pool.tensor_tensor(scale_now[:, r, 1:2], scale_now[:, r, 0:1], y_unit,
                                       ALU.mult).then_inc(s_ready, 1)

            slots(pool, *FFN, slot)
            for r in range(2):
                pool.wait_ge(s_out[r], 16 * ((NT + 1 - r) // 2))

        @block.scalar
        def _(act):
            act.dma_start(gamma_sb, gamma).then_inc(s_gamma, 16)
            for i, (a, b) in enumerate(((0, 2 * D), (2 * D, 3 * D), (3 * D, 6 * D))):
                act.dma_start(wmod_sb[:, :, a:b], wmod[:, :, a:b]).then_inc(s_cmod[i], 16)
            act.wait_ge(s_c, 16)
            act.activation(c_exp, c_sb, ACT.Exp, scale=-1.0).then_inc(s_cexp, 1)

            def hi_piece(k, u, j):
                if (m := matrix_at(k, HI + 1 - u)) is not None:
                    i = 2 * (1 - u) + j
                    if i == 0:
                        act.wait_ge(s_wscale, m + 1)
                        if isinstance(m, int) and m > NM - STAGES:
                            act.wait_ge(s_wlo, m)
                    act.activation(part_piece(m, 0, i), raw_piece(m, i), ACT.Copy,
                                   scale=w_scale[:, bass.ds(m, 1)]).then_inc(s_whi, 1)

            def slot(k, u):
                if it := att_item(k, u, SCORE):
                    n, g, r = it
                    act.wait_ge(s_kx, n + 1)
                    need(act, s_kv, n - 1)
                    act.activation(kg[:, r, :], bank["k"][:, 0:D], ACT.Copy,
                                   scale=decay[:, P - 1:P]).then_inc(s_kg, 1)
                if it := att_item(k, u, NORM2):
                    n, g, r = it
                    act.wait_ge(s_rs2, n + 1)
                    need(act, s_h2, n - 1)
                    act.activation(xn2[:, r, :], x1_sb[:, r, :], ACT.Identity, bias=rs2[:, r, 2:3],
                                   scale=rs2[:, r, 1:2]).then_inc(s_xn2, 1)
                if it := att_item(k, u, PROJ):
                    n, g, r = it
                    act.wait_ge(s_qkp, n + 1)
                    need(act, s_sc, n - 1)
                    need(act, s_qg, n - 1)
                    for h in range(DK):
                        last = act.activation(q_t[:, r, h, :], bank["qk"][:, h * P:(h + 1) * P], ACT.Relu,
                                              bias=bqk_sb[:, 0, h:h + 1])
                    last.then_inc(s_q, 1)
                    for h in range(DK):
                        last = act.activation(k_t[:, r, h, :], bank["qk"][:, D + h * P:D + (h + 1) * P], ACT.Relu,
                                              bias=bqk_sb[:, 1, h:h + 1])
                    last.then_inc(s_k, 1)
                if it := att_item(k, u, XPOSE2):
                    n, g, r = it
                    act.wait_ge(s_h2x, n + 1)
                    need(act, s_lg, n - 1)
                    act.activation(h2_t[:, r], bank["h"][:, 0:D].rearrange("p (k t) -> p k t", k=DK),
                                   ACT.Copy).then_inc(s_h2t, 1)
                hi_piece(k, u, 0)
                if it := att_item(k, u, XPOSE):
                    n, g, r = it
                    act.wait_ge(s_xt, n + 1)
                    if isinstance(n, int) and n == 0:
                        act.wait_ge(s_modt_ready, 1)
                    need(act, s_vp, n - 1)
                    for h in range(DK):
                        last = act.activation(h_t[:, r, h, :], bank["x"][:, h * P:(h + 1) * P], ACT.Identity,
                                              bias=mod_t[:, h, r:r + 1], scale=mod_t[:, DK + h, r:r + 1])
                    last.then_inc(s_ht, 1)
                if it := att_item(k, u, NORM):
                    n, g, r = it
                    act.wait_ge(s_rs1, n + 1)
                    need(act, s_xt, n - 1)
                    act.activation(xn1[:, r, :], x_sb[:, r, bass.ds(g % 4, 1), :].rearrange("p a d -> p (a d)"),
                                   ACT.Identity, bias=rs1[:, r, 2:3], scale=rs1[:, r, 1:2]).then_inc(s_xn1, 1)
                hi_piece(k, u, 1)

            slots(act, *ATT, slot)

            act.wait_ge(s_minus, 1)
            for i in range(ACT_CHUNKS):
                n = NCH - ACT_CHUNKS + i
                last = act.activation(distance[:, i, :], con("slot_no"), ACT.Abs, bias=minus_slot[:, n:n + 1])
            last.then_inc(s_distance, 1)
            act.wait_ge(s_distance, 1)
            act.activation(in_slot[:, NCH - ACT_CHUNKS:NCH, :], distance, ACT.Relu, bias=con("ones")[:, 0:1],
                           scale=-1.0).then_inc(s_act_bits, 1)

            act.wait_ge(s_idx, 1)

            def hidden(n, r, h):
                act.wait_ge(s_hp, 2 * n + h + 1)
                act.wait_ge(s_ready, n + 1)
                need(act, s_hlo, 2 * n + h - 1)
                for f in range(4 * h, 4 * h + 4):
                    last = act.activation(hid[:, f, :], bank[("qk", "va")[h]][:, (f % 4) * P:(f % 4 + 1) * P],
                                          ACT.Relu, bias=b1_now[:, r, f:f + 1], scale=HID_SCALE)
                last.then_inc(s_ha, 1)

            def hidden_hi(n, r, h):
                act.wait_ge(s_ha, 2 * n + h + 1)
                need(act, s_y, n - 1)
                act.activation(hid_parts[:, r % 2, 0, 4 * h:4 * h + 4, :], hid[:, 4 * h:4 * h + 4, :],
                               ACT.Copy).then_inc(s_hhi, 1)

            def slot(k, u):
                if it := ffn_item(k, u, -1):
                    n, g, r = it
                    if isinstance(n, int) and n == 0:
                        act.wait_ge(s_routed, 1)
                    need(act, s_gate, n - 1)
                    act.activation(gate_part[:, r % 2, 0, :], gate_b[:, 0, :], ACT.Copy,
                                   scale=slot_early[:, bass.ds(n, 1)])
                    act.activation(gate_part[:, r % 2, 1, :], gate_b[:, 1, :], ACT.Copy,
                                   scale=slot_late[:, bass.ds(n, 1)]).then_inc(s_gpart, 1)
                if it := ffn_item(k, u, 0):
                    hidden(it[0], it[2], 0)
                    hidden_hi(it[0], it[2], 0)
                if it := ffn_item(k, u, -1):
                    n, g, r = it
                    act.wait_ge(s_tx, n + 1)
                    need(act, s_hp, 2 * (n - 1))
                    act.activation(tok_parts[:, r % 2, 0], bank["h"][:, 0:D].rearrange("p (k t) -> p k t", k=DK),
                                   ACT.Copy, scale=x_scale).then_inc(s_thi, 1)
                if it := ffn_item(k, u, 0):
                    hidden(it[0], it[2], 1)
                    hidden_hi(it[0], it[2], 1)

            slots(act, *FFN, slot)

        @block.vector
        def _(dve):
            steps = [0]

            def step(ins):
                steps[0] += 1
                ins.then_inc(s_setup, 1)
                dve.wait_ge(s_setup, steps[0])

            dve.wait_ge(s_cexp, 1)
            step(dve.tensor_scalar(c_exp, c_exp, 1.0, None, ALU.add))
            step(dve.reciprocal(c_exp, c_exp))
            step(dve.tensor_tensor(c_silu, c_sb, c_exp, ALU.mult))
            dve.memset(small[:, 50:51], 0.0).then_inc(s_csilu, 1)
            dve.memset(x_most, 0.0).then_inc(s_xbound, 1)

            def powers():
                dve.wait_ge(s_const, 16)
                dve.wait_ge(s_gamma, 16)
                step(dve.tensor_tensor_scan(decay[:], gamma_sb.to_broadcast([P, P]), con("ident"), 0.0,
                                            ALU.mult, ALU.add))
                dve.tensor_tensor_scan(power[:], gamma_sb.to_broadcast([P, P]), con("ones"), 1.0,
                                       ALU.mult, ALU.mult).then_inc(s_decay, 1)
                dve.wait_ge(s_decay, 1)

            def first_stats(k, u):
                if it := att_item(k, u, STATS):
                    n, g, r = it
                    dve.wait_ge(s_x[r], 16 * (g + 1))
                    dve.bn_stats(st1[:, r, :], x_sb[:, r, g % 4, :]).then_inc(s_st1, 1)

            def first_mean_var(k, u):
                if it := att_item(k, u, STATS):
                    n, g, r = it
                    need(dve, s_rs1, n - 1)
                    dve.wait_ge(s_st1, n + 1)
                    dve.bn_aggr(mv1[:, r, :], st1[:, r, :]).then_inc(s_mv1, 1)

            def mod_widths():
                dve.wait_ge(s_modt, 1)
                m = bank["k"][:, 0:4 * B].rearrange("p (m b) -> p m b", b=B)
                dve.tensor_copy(mod_t[:, 0:DK, :], m[:, 0:DK, :])
                dve.tensor_scalar(mod_t[:, DK:2 * DK, :], m[:, DK:2 * DK, :], 1.0, None,
                                  ALU.add).then_inc(s_modt_ready, 1)

            def gate(to, src):
                step(dve.tensor_copy(raw_sb, src))
                step(dve.tensor_scalar(sign_sb, raw_sb, 0.0, 2.0, ALU.is_ge, ALU.mult))
                step(dve.scalar_tensor_tensor(mag_sb, raw_sb, -1.0, raw_sb, ALU.mult, ALU.max))
                step(dve.tensor_scalar(mag_sb, mag_sb, 0.25, None, ALU.max))
                return dve.scalar_tensor_tensor(to, sign_sb, -1.0, mag_sb, ALU.add, ALU.mult)

            def first_gate():
                dve.wait_ge(s_modb, 1)
                gate(mod2_sb[:, 0:D], bank["o"][0:B, 0:D]).then_inc(s_modb_ready, 1)
                dve.wait_ge(s_modb_ready, 1)

            def other_rows():
                dve.wait_ge(s_modb, 2)
                dve.tensor_copy(mod2_sb[:, D:2 * D], bank["h"][0:B, 0:D])
                dve.tensor_scalar(mod2_sb[:, 2 * D:3 * D], bank["h"][0:B, D:2 * D], 1.0, None, ALU.add)
                step(gate(mod2_sb[:, 3 * D:4 * D], bank["kv1"][0:B, 0:D]))
                dve.wait_ge(s_xbound, 1)
                dve.tensor_reduce(x_most[0:B, 0:1], mod2_sb[:, 2 * D:3 * D], AX_X, ALU.max, apply_absolute_value=True)
                dve.tensor_reduce(x_most[0:B, 1:2], mod2_sb[:, D:2 * D], AX_X, ALU.max,
                                  apply_absolute_value=True).then_inc(s_xmost, 1)
                dve.memset(small[:, 51:52], 0.0).then_inc(s_modb_ready, 1)

            def b1_bound():
                dve.wait_ge(s_misc, 64)
                dve.tensor_reduce(b1_max, b1_sb[:], AX_X, ALU.max, apply_absolute_value=True).then_inc(s_bound, 1)

            def scale_of(largest, scale, unscale, s_step, base, s_to):
                dve.tensor_scalar(bits.bitcast(I32), largest.bitcast(I32), EXPONENT, None,
                                  ALU.bitwise_and).then_inc(s_step, 1)
                dve.wait_ge(s_step, base + 1)
                dve.tensor_scalar(scale.bitcast(I32), bits.bitcast(I32), -1.0, float((TOP + 254) * EXP_ONE),
                                  ALU.mult, ALU.add)
                dve.tensor_scalar(unscale.bitcast(I32), bits.bitcast(I32), float(-TOP * EXP_ONE), None,
                                  ALU.add).then_inc(s_to, 1)

            def token_scale():
                dve.wait_ge(s_xall, 1)
                step(dve.scalar_tensor_tensor(x_most[:, 2:3], x_all[:, 0:1], float(D) ** 0.5, x_all[:, 1:2],
                                              ALU.mult, ALU.add))
                step(dve.tensor_scalar(x_most[:, 3:4], x_most[:, 2:3], 2.0 ** -60, None, ALU.max))
                scale_of(x_most[:, 3:4], x_scale, x_unscale, s_xstep, 0, s_xscale)
                dve.wait_ge(s_xscale, 1)
                step(dve.tensor_scalar(hid_unit, x_scale, HID_SCALE, None, ALU.mult))
                step(dve.tensor_scalar(y_unit, x_unscale, 1.0 / HID_SCALE, None, ALU.mult))
                step(dve.memset(w_floor[:], 2.0 ** -60))
                dve.wait_ge(s_bmax, 1)
                step(dve.tensor_scalar(w_floor[:, 0:NM:2], b1_all, hid_unit, 2.0, ALU.mult, ALU.mult))
                step(dve.tensor_scalar(w_floor[:], w_floor[:], 2.0 ** -60, None, ALU.max))

            def consts16():
                dve.tensor_copy(c16[:, 0:P], con("before"))
                dve.tensor_copy(c16[:, P:2 * P], con("ones"))
                step(dve.tensor_copy(c16[:, 2 * P:3 * P + NT], cst[:, COLS["slot_no"][0]:COLS["tile_no"][1]]))

            def max_piece(k, u, j):
                if (m := matrix_at(k, MAX)) is None:
                    return
                i = 2 * u + j
                if i == 0:
                    dve.wait_ge(s_wraw, 16 * (m + 1))
                last = dve.tensor_reduce(piece_max[:, i:i + 1], raw_piece(m, i), AX_X, ALU.max,
                                         apply_absolute_value=True)
                if i == PIECES - 1:
                    last.then_inc(s_wmaxh, 1)
                    dve.wait_ge(s_wmaxh, m + 1)
                    dve.tensor_reduce(lane_max, piece_max, AX_X, ALU.max).then_inc(s_wboth, 1)

            def lo_piece(k, u, j):
                if (m := matrix_at(k, LO)) is None:
                    return
                i = 2 * u + j
                dve.wait_ge(s_whi, PIECES * m + i + 1)
                last = dve.scalar_tensor_tensor(part_piece(m, 1, i), raw_piece(m, i), w_scale[:, bass.ds(m, 1)],
                                                part_piece(m, 0, i), ALU.mult, ALU.subtract)
                if i == PIECES - 1:
                    last.then_inc(s_wlo, 1)

            hops = [0]

            def hop(ins):
                hops[0] += 1
                ins.then_inc(s_route, 1)
                dve.wait_ge(s_route, hops[0])

            def choose(a, b):
                dve.wait_ge(s_lgr, b)
                shape = [P, b - a, NE]
                hop(dve.tensor_reduce(top[:, a:b], logits[:, a:b], AX_X, ALU.max))
                hop(dve.tensor_tensor(hot[:, a:b], logits[:, a:b], top[:, a:b].unsqueeze(2).to_broadcast(shape),
                                      ALU.is_equal))
                hop(dve.tensor_tensor(hot[:, a:b], hot[:, a:b], con("weight8").unsqueeze(1).to_broadcast(shape),
                                      ALU.mult))
                hop(dve.tensor_reduce(best[:, a:b], hot[:, a:b], AX_X, ALU.max))
                return dve.tensor_tensor(chosen_ne[:, a:b], hot[:, a:b], best[:, a:b].unsqueeze(2).to_broadcast(shape),
                                         ALU.is_equal)

            def slot(k, u):
                attend, score = att_item(k, u, ATTEND), att_item(k, u, SCORE)
                if attend:
                    n, g, r = attend
                    if n == 0:
                        dve.wait_ge(s_modl, 16)
                    dve.wait_ge(s_o, n + 1)
                    dve.tensor_scalar(den[:, r, 0:1], bank["o"][:, D:DZ], DEN_EPS, None, ALU.add).then_inc(s_den, 1)
                first_stats(k, u)
                if attend:
                    dve.wait_ge(s_den, n + 1)
                    dve.reciprocal(den[:, r, 1:2], den[:, r, 0:1]).then_inc(s_rden, 1)
                lo_piece(k, u, 0)
                if attend:
                    dve.wait_ge(s_rden, n + 1)
                    dve.scalar_tensor_tensor(attended[:, r, :], bank["o"][:, 0:D], den[:, r, 1:2], gate_a[:, r, :],
                                             ALU.mult, ALU.mult).then_inc(s_atn, 1)
                first_mean_var(k, u)
                if score:
                    n = score[0]
                    dve.wait_ge(s_sc, n + 1)
                    need(dve, s_o, n - 1)
                    dve.tensor_tensor(att[:, score[2], :], bank["va"][:, D:D + P], decay[:], ALU.mult).then_inc(s_att, 1)
                if attend:
                    n, g, r = attend
                    dve.wait_ge(s_atn, n + 1)
                    need(dve, s_sx[r], 16 * g)
                    need(dve, s_xn2, n - 1)
                    dve.tensor_tensor(x1_sb[:, r, :], attended[:, r, :], x_sb[:, r, g % 4, :],
                                      ALU.add).then_inc(s_x1, 1)
                    dve.wait_ge(s_kv, n + 1)
                    for h in range(DK):
                        last = dve.scalar_tensor_tensor(state[:, r, h, 0:DZ], state[:, r, h, 0:DZ],
                                                        power[:, P - 1:P], bank[f"kv{h}"][:, 0:DZ],
                                                        ALU.mult, ALU.add)
                    last.then_inc(s_state, 1)
                    dve.wait_ge(s_x1, n + 1)
                    dve.bn_stats(st2[:, r, :], x1_sb[:, r, :]).then_inc(s_st2, 1)
                max_piece(k, u, 0)
                if attend:
                    need(dve, s_rs2, n - 1)
                    dve.wait_ge(s_st2, n + 1)
                    dve.bn_aggr(mv2[:, r, :], st2[:, r, :]).then_inc(s_mv2, 1)
                if it := att_item(k, u, LOGIT):
                    n, g, r = it
                    if n == NCH - 1:
                        hop(choose(0, n))
                    dve.wait_ge(s_lg, n + 1)
                    dve.tensor_tensor(logits[:, n, :], bank["h"][:, D:D + NE], br_sb[:], ALU.add).then_inc(s_lgr, 1)
                if it := att_item(k, u, PROJ):
                    n, g, r = it
                    dve.wait_ge(s_vp, n + 1)
                    if n == 0:
                        dve.wait_ge(s_init, INIT)
                    need(dve, s_kv, n - 1)
                    dve.tensor_tensor(v_ext[:, r, 0:D], bank["va"][:, 0:D], bv_sb[:], ALU.add).then_inc(s_v, 1)
                lo_piece(k, u, 1)
                if (k, u) == (1, 0):
                    token_scale()
                if (k, u) == (2, 0):
                    consts16()
                if u == 0 and (m := matrix_at(k, HI)) is not None:
                    dve.wait_ge(s_wmax, m + 1)
                    dve.tensor_tensor(w_most, all_max, w_floor[:, m:m + 1], ALU.max).then_inc(s_wfloor, 1)
                    dve.wait_ge(s_wfloor, m + 1)
                    scale_of(w_most, w_scale[:, m:m + 1], w_unscale[:, m:m + 1], s_wbits, m, s_wscale)
                if (k, u) == (-2, 1):
                    mod_widths()
                    powers()
                if (k, u) == (-1, 1):
                    first_gate()
                if (k, u) == (0, 1):
                    other_rows()
                    b1_bound()
                max_piece(k, u, 1)

            slots(dve, *ATT_S, slot)

            upto = scratch[:, 640:640 + NE * NCH + 1]
            count = scratch[:, 900:900 + NE]
            full = scratch[:, 908:908 + NE]
            upto_tile = scratch[:, 916:916 + NE]
            first = scratch[:, 924:924 + NE]
            count_i = scratch[:, 932:932 + NE].bitcast(I32)
            place = scratch[:, 1280:1536]
            pos = scratch[:, 1536:1568]
            pos_i = scratch[:, 1568:1600].bitcast(I32)
            pos_tile = scratch[:, 1600:1632].bitcast(I32)
            pos_slot_i = scratch[:, 1632:1664].bitcast(I32)
            pos_slot = scratch[:, 1664:1696]
            late = scratch[:, 1696:1696 + NT * NE].rearrange("p (t e) -> p t e", e=NE)
            tile_f = scratch[:, 2016:2016 + NT]
            token_f = scratch[:, 2056:2056 + NT]

            choose(NCH - 1, NCH).then_inc(s_chosen, 1)
            for b in range(B):
                dve.wait_ge(s_sx[b], 16 * (NCH // B))
                dve.wait_ge(s_sh[b], 16 * (NCH // B))
            dve.memset(upto[:, 0:1], 0.0).then_inc(s_start, 1)
            dve.wait_ge(s_start, 1)
            dve.wait_ge(s_rank, 1)
            one = con("ones")[:, 0:1]
            hop(dve.tensor_tensor_scan(upto[:, 1:1 + NE * NCH], one.to_broadcast([P, NE * NCH]), bank["va"][:, 0:NE * NCH], 0.0,
                                       ALU.mult, ALU.add))
            ends = upto[:, NCH:NE * NCH + 1:NCH]
            starts = upto[:, 0:NE * NCH:NCH]
            hop(dve.tensor_tensor(count, ends, starts, ALU.subtract))
            hop(dve.tensor_scalar(count_i, count, float(P - 1), None, ALU.add))
            hop(dve.tensor_scalar(count_i, count_i, 7, None, ALU.arith_shift_right))
            hop(dve.tensor_copy(full, count_i))
            hop(dve.tensor_tensor_scan(upto_tile, one.to_broadcast([P, NE]), full, 0.0,
                                       ALU.mult, ALU.add))
            hop(dve.tensor_tensor(first, upto_tile, full, ALU.subtract))
            hop(dve.scalar_tensor_tensor(first, first, float(P), starts, ALU.mult, ALU.subtract))
            hop(dve.tensor_tensor(place, bank["qk"][:, 0:NE * NCH], upto[:, 0:NE * NCH], ALU.add))
            place_en = place.rearrange("p (e n) -> p e n", e=NE)
            hop(dve.tensor_tensor(place_en, place_en, first.unsqueeze(2).to_broadcast([P, NE, NCH]), ALU.add))
            hop(dve.tensor_tensor(place, place, chosen16, ALU.mult))
            hop(dve.tensor_reduce(pos, place.rearrange("p (e n) -> p n e", e=NE), AX_X, ALU.add))
            hop(dve.tensor_copy(pos_i, pos))
            dve.tensor_scalar(pos_tile, pos_i, 7, None, ALU.arith_shift_right)
            hop(dve.tensor_scalar(pos_slot_i, pos_i, P - 1, None, ALU.bitwise_and))
            dve.tensor_tensor(hot_tile, pos_tile.unsqueeze(2).to_broadcast([P, NCH, NT]),
                              con("tile_no").unsqueeze(1).to_broadcast([P, NCH, NT]), ALU.is_equal).then_inc(s_hot, 1)
            dve.tensor_scalar(minus_slot, pos_slot_i, -1.0, None, ALU.mult).then_inc(s_minus, 1)
            hop(dve.tensor_copy(pos_slot, pos_slot_i))
            dve.wait_ge(s_hot, 1)
            dve.tensor_scalar(in_tile[:, :, 1, :], hot_tile, con("lane"), None, ALU.mult)
            for n in range(NCH - ACT_CHUNKS):
                last = dve.tensor_scalar(in_slot[:, n, :], slot_no16, pos_slot[:, n:n + 1], None, ALU.is_equal)
                if n % 8 == 7:
                    last.then_inc(s_bits, 1)
            hop(dve.tensor_tensor(late[:, :, 0:NE - 1], con("tile_no").unsqueeze(2).to_broadcast([P, NT, NE - 1]),
                                  upto_tile[:, 0:NE - 1].unsqueeze(1).to_broadcast([P, NT, NE - 1]), ALU.is_ge))
            hop(dve.tensor_reduce(tile_f, late[:, :, 0:NE - 1], AX_X, ALU.add))
            hop(dve.tensor_scalar(tile_matrix[:], tile_f, 2.0, None, ALU.mult))
            dve.wait_ge(s_ids, 1)
            hop(dve.tensor_scalar(token_f, bank["x"][:, 0:NT], float(P), float(NTOK), ALU.mult, ALU.add))
            hop(dve.tensor_tensor(token_f, token_f, bank["x"][:, NT:2 * NT], ALU.add))
            dve.tensor_copy(slot_token[:], token_f).then_inc(s_tokens, 1)
            dve.tensor_scalar(slot_late[:], token_f, float(S), None, ALU.is_ge)
            dve.tensor_scalar(slot_early[:], token_f, float(S), None, ALU.is_lt).then_inc(s_routed, 1)

            dve.wait_ge(s_idx, 1)
            dve.wait_ge(s_b2, 16)

            def hidden_lo(n, r, h):
                dve.wait_ge(s_hhi, 2 * n + h + 1)
                dve.tensor_tensor(hid_parts[:, r % 2, 1, 4 * h:4 * h + 4, :], hid[:, 4 * h:4 * h + 4, :],
                                  hid_parts[:, r % 2, 0, 4 * h:4 * h + 4, :], ALU.subtract).then_inc(s_hlo, 1)

            def last_tile(it):
                return isinstance(it[0], int) and it[0] == NT - 1

            def copy_w1(m, n, i):
                if i == 1:
                    need(dve, s_hp, 2 * n)
                of = w[:, bass.ds(m, 1)].rearrange("p a i (h f) -> p (a i h) f", h=DK)
                now = w1_now.rearrange("p i (h f) -> p (i h) f", h=DK)
                dve.tensor_copy(now[:, :, i * F // 2:(i + 1) * F // 2],
                                of[:, :, i * F // 2:(i + 1) * F // 2]).then_inc(s_w1, 1)

            def slot(k, u):
                if it := ffn_item(k, u, -1):
                    alone(dve, (s_hp, 2 * it[0] - 1))
                    m = dve.value_load(tile_matrix[0:1, bass.ds(it[0], 1)], min_val=0, max_val=NM - 2)
                    copy_w1(m, it[0], 0)
                    if cur := ffn_item(k, u, 0):
                        hidden_lo(cur[0], cur[2], 0)
                    copy_w1(m, it[0], 1)
                    n, g, r = it
                    dve.wait_ge(s_thi, n + 1)
                    dve.scalar_tensor_tensor(tok_parts[:, r % 2, 1],
                                             bank["h"][:, 0:D].rearrange("p (k t) -> p k t", k=DK), x_scale,
                                             tok_parts[:, r % 2, 0], ALU.mult, ALU.subtract).then_inc(s_tlo, 1)
                if it := ffn_item(k, u, 0):
                    if last_tile(it):
                        hidden_lo(it[0], it[2], 0)
                    hidden_lo(it[0], it[2], 1)
                if it := ffn_item(k, u, 1):
                    n, g, r = it
                    alone(dve, (s_out[r % 2], 16 * (2 * g + r // 2)), (s_y, n + 1))
                    m = dve.value_load(tile_matrix[0:1, bass.ds(n, 1)], min_val=0, max_val=NM - 2)
                    b2_of = b2_sb[:].rearrange("p e (a d) -> p (e a) d", a=2)[:, bass.ds(m, 2), :]
                    dve.scalar_tensor_tensor(done_rows[:, r % 2, :], bank["o"][:, 0:D], scale_now[:, r, 1:2],
                                             b2_of.rearrange("p a d -> p (a d)"), ALU.mult, ALU.add).then_inc(s_ys, 1)
                    dve.wait_ge(s_gate, n + 1)
                    dve.wait_ge(s_ys, 2 * n + 1)
                    dve.tensor_tensor(done_rows[:, r % 2, :], done_rows[:, r % 2, :], gate_now[:, r, :],
                                      ALU.mult).then_inc(s_ys, 1)

            slots(dve, *FFN, slot)

        @block.tensor
        def _(pe):
            pe.wait_ge(s_csilu, 1)
            pe.wait_ge(s_cmod[0], 16)
            for m in range(2 * DK):
                for k in range(DK):
                    last = pe.matmul(bank["k"][:, m * B:(m + 1) * B], wmod_sb[:, k, m * P:(m + 1) * P],
                                     c_silu[:, k, :], start=(k == 0), stop=(k == DK - 1))
            last.then_inc(s_modt, 1)

            def mod_rows(name, a, b):
                for k in range(DK):
                    last = pe.matmul(bank[name][0:B, 0:b - a], c_silu[:, k, :], wmod_sb[:, k, a:b],
                                     start=(k == 0), stop=(k == DK - 1))
                return last

            def slot(k, u):
                if it := att_item(k, u, ATTEND):
                    n, g, r = it
                    if isinstance(n, int) and n == 0:
                        pe.wait_ge(s_init, INIT)
                        pe.wait_ge(s_modb_ready, 1)
                    pe.wait_ge(s_att, n + 1)
                    pe.wait_ge(s_v, n + 1)
                    need(pe, s_atn, n)
                    pe.matmul(bank["o"][:, 0:DZ], att[:, r, :], v_ext[:, r, 0:DZ], start=True, stop=False)
                    pe.wait_ge(s_qg, n + 1)
                    need(pe, s_state, n - 1)
                    for h in range(DK):
                        last = pe.matmul(bank["o"][:, 0:DZ], qg_t[:, r, h, :], state[:, r, h, 0:DZ],
                                         start=False, stop=(h == DK - 1))
                    last.then_inc(s_o, 1)
                    if isinstance(n, int) and n == 0:
                        pe.wait_ge(s_modb_ready, 2)
                    pe.wait_ge(s_kg, n + 1)
                    need(pe, s_state, n)
                    for h in range(DK):
                        last = pe.matmul(bank[f"kv{h}"][:, 0:DZ], kg[:, r, h * P:(h + 1) * P], v_ext[:, r, 0:DZ],
                                         start=True, stop=True)
                    last.then_inc(s_kv, 1)
                if it := att_item(k, u, LOGIT):
                    n, g, r = it
                    pe.wait_ge(s_h2t, n + 1)
                    for h in range(DK):
                        last = pe.matmul(bank["h"][:, D:D + NE], h2_t[:, r, h, :], wr_sb[:, h, :],
                                         start=(h == 0), stop=(h == DK - 1))
                    last.then_inc(s_lg, 1)
                if it := att_item(k, u, SCORE):
                    n, g, r = it
                    pe.wait_ge(s_k, n + 1)
                    need(pe, s_kg, n)
                    for h in range(DK):
                        last = pe.transpose(bank["k"][:, h * P:(h + 1) * P], k_t[:, r, h, :], ident)
                    last.then_inc(s_kx, 1)
                    pe.wait_ge(s_v, n + 1)
                    for h in range(DK):
                        last = pe.matmul(bank["va"][:, D:D + P], k_t[:, r, h, :], q_t[:, r, h, :],
                                         start=(h == 0), stop=(h == DK - 1))
                    last.then_inc(s_sc, 1)
                if it := att_item(k, u, PROJ):
                    n, g, r = it
                    if isinstance(n, int) and n == 0:
                        pe.wait_ge(s_wqkv, 32)
                    pe.wait_ge(s_ht, n + 1)
                    need(pe, s_k, n)
                    for m in range(2):
                        for c in range(DK):
                            for h in range(DK):
                                last = pe.matmul(bank["qk"][:, (m * DK + c) * P:(m * DK + c + 1) * P],
                                                 wqkv_sb[:, m, h, c * P:(c + 1) * P], h_t[:, r, h, :],
                                                 start=(h == 0), stop=(h == DK - 1))
                    last.then_inc(s_qkp, 1)
                    need(pe, s_att, n)
                    for h in range(DK):
                        last = pe.matmul(bank["va"][:, 0:D], h_t[:, r, h, :], wqkv_sb[:, 2, h, :],
                                         start=(h == 0), stop=(h == DK - 1))
                    last.then_inc(s_vp, 1)
                if it := att_item(k, u, XPOSE2):
                    n, g, r = it
                    pe.wait_ge(s_h2, n + 1)
                    need(pe, s_h2t, n)
                    need(pe, s_lgr, n)
                    for h in range(DK):
                        last = pe.transpose(bank["h"][:, h * P:(h + 1) * P], h2[:, r, h * P:(h + 1) * P], ident)
                    last.then_inc(s_h2x, 1)
                if it := att_item(k, u, XPOSE):
                    n, g, r = it
                    if isinstance(n, int) and n == 0:
                        pe.wait_ge(s_const, 16)
                    pe.wait_ge(s_xn1, n + 1)
                    need(pe, s_ht, n)
                    for h in range(DK):
                        last = pe.transpose(bank["x"][:, h * P:(h + 1) * P], xn1[:, r, h * P:(h + 1) * P], ident)
                    last.then_inc(s_xt, 1)
                if isinstance(k, int) and (k, u) == (-1, 1):
                    pe.wait_ge(s_cmod[1], 16)
                    mod_rows("o", 2 * D, 3 * D).then_inc(s_modb, 1)
                if isinstance(k, int) and (k, u) == (0, 0):
                    pe.wait_ge(s_cmod[2], 16)
                    mod_rows("h", 3 * D, 5 * D)
                    mod_rows("kv1", 5 * D, 6 * D).then_inc(s_modb, 1)
            slots(pe, *ATT, slot)

            pe.wait_ge(s_chosen, 1)
            pe.matmul(bank["qk"][:, 0:NE * NCH], before16, chosen16, start=True, stop=True)
            pe.matmul(bank["va"][:, 0:NE * NCH], ones16, chosen16, start=True, stop=True).then_inc(s_rank, 1)
            for n in range(NCH):
                if n == 0:
                    pe.wait_ge(s_numbers, 1)
                if n == NCH - ACT_CHUNKS:
                    pe.wait_ge(s_act_bits, 1)
                elif n % 8 == 0:
                    pe.wait_ge(s_bits, n // 8 + 1)
                last = pe.matmul(bank["x"][:, 0:2 * NT], in_slot[:, n, :],
                                 in_tile[:, n].rearrange("p i t -> p (i t)"), start=(n == 0), stop=(n == NCH - 1))
            last.then_inc(s_ids, 1)

            pe.wait_ge(s_routed, 1)
            pe.wait_ge(s_wlo, NM)

            parts = ((0, 0), (0, 1), (1, 0))

            def slot(k, u):
                if it := ffn_item(k, u, 0):
                    n, g, r = it
                    pe.wait_ge(s_tlo, n + 1)
                    for i, name in enumerate(("qk", "va")):
                        pe.wait_ge(s_w1, 2 * n + i + 1)
                        need(pe, s_ha, 2 * n + i - 1)
                        for f in range(4 * i, 4 * i + 4):
                            for q, (a, b) in enumerate(parts):
                                for h in range(DK):
                                    at_w = h * F + f * P
                                    last = pe.matmul(bank[name][:, (f % 4) * P:(f % 4 + 1) * P],
                                                     w1_now[:, a, at_w:at_w + P], tok_parts[:, r % 2, b, h, :],
                                                     start=(q == 0 and h == 0), stop=(q == 2 and h == DK - 1))
                        last.then_inc(s_hp, 1)
                if it := ffn_item(k, u, -1):
                    n, g, r = it
                    pe.wait_ge(s_in[r], 16 * (g + 1))
                    need(pe, s_tlo, n)
                    for h in range(DK):
                        last = pe.transpose(bank["h"][:, h * P:(h + 1) * P],
                                            tok[:, r, D + h * P:D + (h + 1) * P], ident)
                    last.then_inc(s_tx, 1)
                if it := ffn_item(k, u, 1):
                    n, g, r = it
                    m = pe.value_load(tile_matrix[0:1, bass.ds(n, 1)], min_val=0, max_val=NM - 2)
                    pe.wait_ge(s_hlo, 2 * n + 2)
                    need(pe, s_ys, 2 * n - 1)
                    for f in range(FK):
                        for q, (a, b) in enumerate(parts):
                            last = pe.matmul(bank["o"][:, 0:D], hid_parts[:, r % 2, b, f, :],
                                             w[:, bass.ds(m + 1, 1), a, f * D:(f + 1) * D].rearrange("p a d -> p (a d)"),
                                             start=(f == 0 and q == 0), stop=(f == FK - 1 and q == 2))
                    last.then_inc(s_y, 1)

            slots(pe, *FFN, slot)


def kernel(L0_attn_x_seq, L0_attn_Wq, L0_attn_bq, L0_attn_Wk, L0_attn_bk, L0_attn_Wv, L0_attn_bv, L0_attn_gamma,
           L0_ffn_Wr, L0_ffn_br, L0_ffn_W1, L0_ffn_b1, L0_ffn_W2, L0_ffn_b2, L0_c, L0_wmod):
    import concourse.bacc as bacc
    from concourse.bass_utils import run_bass_kernel_spmd

    def by_width(a):
        a = np.asarray(a)
        return np.moveaxis(a.reshape(*a.shape[:-1], -1, P), -1, 0)

    def rows_of(a, shape):
        return np.broadcast_to(np.asarray(a).reshape(1, -1), (P, int(np.prod(shape)))).reshape(P, *shape)

    qkv = np.stack([np.asarray(w) for w in (L0_attn_Wq, L0_attn_Wk, L0_attn_Wv)])
    consts = constants()
    laid = {
        "x": np.asarray(L0_attn_x_seq).reshape(NTOK, D),
        "wqkv": by_width(qkv).transpose(0, 1, 3, 2),
        "bqk": by_width(np.stack([np.asarray(L0_attn_bq), np.asarray(L0_attn_bk)])),
        "bvb": rows_of(L0_attn_bv, (D,)),
        "gamma": rows_of(L0_attn_gamma, (1,)),
        "wr": by_width(L0_ffn_Wr).transpose(0, 2, 1),
        "brb": rows_of(L0_ffn_br, (NE,)),
        "w_raw": np.stack([
            by_width(L0_ffn_W1).transpose(1, 0, 3, 2).reshape(NE, P, MW),
            by_width(L0_ffn_W2).transpose(1, 0, 3, 2).reshape(NE, P, MW),
        ], 1).reshape(NM, P, MW),
        "b1": by_width(L0_ffn_b1),
        "b2b": rows_of(L0_ffn_b2, (NE, D)),
        "c_t": by_width(L0_c).transpose(0, 2, 1),
        "wmod": np.asarray(L0_wmod).reshape(DK, P, 6 * D).transpose(1, 0, 2),
        "consts": consts,
    }
    nc = bacc.Bacc("TRN2", target_bir_lowering=False, num_devices=1)
    arrays, args = {}, []
    for name, a in laid.items():
        a = np.ascontiguousarray(a)
        arrays[f"in_{name}"] = a
        args.append(nc.dram_tensor(f"in_{name}", a.shape, mybir.dt.from_np(a.dtype), kind="ExternalInput").ap())
    args.append(nc.dram_tensor("out_rows", (NTOK, D), F32, kind="ExternalOutput").ap())
    build(nc, *args)
    r = run_bass_kernel_spmd(nc, [arrays], core_ids=[0])
    return r.results[0]["out_rows"].reshape(B, S, D)
```
